# Optimizing a Trainium2 kernel written in Bass

```python
import numpy as np
import jax
import jax.numpy as jnp

def _softmax(x, axis=-1):
    return jax.nn.softmax(x, axis=axis)

def _gelu(x):
    return jax.nn.gelu(x, approximate=True)

def _silu(x):
    return jax.nn.silu(x)

def _sigmoid(x):
    return jax.nn.sigmoid(x)

def _layernorm(x, axis=-1, eps=1e-05):
    m = jnp.mean(x, axis=axis, keepdims=True)
    v = jnp.var(x, axis=axis, keepdims=True)
    return (x - m) / jnp.sqrt(v + eps)

def _scatter_add(tgt, idx, src, axis=0):
    return tgt.at[idx].add(src)

def _segment_sum(src, seg, n):
    return jax.ops.segment_sum(src, seg, n)
kernel_name = 'mk_vit_tower_d1_tok_img256_r4_5933b8'

def setup_inputs(seed: int=0):
    np.random.seed(seed)
    _w = jnp.asarray

    def _rec_inputs():
        import jax
        import jax.numpy as jnp
        _rk = jax.random.key(seed)
        x = -0.0003702 + 0.999946 * jax.random.normal(jax.random.fold_in(_rk, 1), (64, 1, 96, 96), jnp.float32)
        return x
    x = _rec_inputs()

    def _L0_tok_setup():
        import jax, jax.numpy as jnp
        import numpy as np
        PH, PW = (64, 25)
        SH, SW = (64, 12)

        def _unfold(x, ph, pw, sh, sw):
            B, C, H, W = x.shape
            nh = (H - ph) // sh + 1
            nw = (W - pw) // sw + 1
            rows = jnp.arange(nh)[:, None] * sh + jnp.arange(ph)[None, :]
            cols = jnp.arange(nw)[:, None] * sw + jnp.arange(pw)[None, :]
            p = x[:, :, rows, :]
            p = p[:, :, :, :, cols]
            p = jnp.transpose(p, (0, 2, 4, 1, 3, 5))
            return p.reshape(B, nh * nw, C * ph * pw)
        key = jax.random.key(seed)
        kx, kw = jax.random.split(key, 2)
        x = jax.random.normal(kx, (64, 1, 64, 1000), dtype=jnp.float32)
        in_dim = 1 * PH * PW
        weight = jax.random.normal(kw, (in_dim, 64), dtype=jnp.float32) / np.sqrt(in_dim).astype(np.float32)
        bias = jnp.zeros((64,), dtype=jnp.float32)
        return {'x': x, 'weight': weight, 'bias': bias}
    _L0_tok_all = _L0_tok_setup()
    _L0_tok_in = {k: v for k, v in _L0_tok_all.items() if k in ('weight', 'bias')}
    del _L0_tok_all

    def _L0_attn_setup():
        import jax, jax.numpy as jnp
        import numpy as np
        SEQ_LEN = 512
        EMBED_DIM = 64
        BATCH = 8
        LN_EPS = 1e-05

        def _layernorm(x, g, b):
            mu = jnp.mean(x, axis=-1, keepdims=True)
            var = jnp.mean(jnp.square(x - mu), axis=-1, keepdims=True)
            return (x - mu) * jax.lax.rsqrt(var + LN_EPS) * g + b
        key = jax.random.key(seed)
        ks = jax.random.split(key, 8)
        C = EMBED_DIM
        x = jax.random.normal(ks[0], (BATCH, SEQ_LEN, C), dtype=jnp.float32)
        qkv_w = jax.random.normal(ks[1], (C, 3 * C), dtype=jnp.float32) * 0.02
        qkv_b = jnp.zeros((3 * C,), dtype=jnp.float32)
        proj_w = jax.random.normal(ks[2], (C, C), dtype=jnp.float32) * 0.02
        proj_b = jnp.zeros((C,), dtype=jnp.float32)
        ln1_g = jnp.ones((C,), dtype=jnp.float32)
        ln1_b = jnp.zeros((C,), dtype=jnp.float32)
        ln2_g = jnp.ones((C,), dtype=jnp.float32)
        ln2_b = jnp.zeros((C,), dtype=jnp.float32)
        bias_table = jax.random.truncated_normal(ks[3], -2.0, 2.0, (2 * SEQ_LEN - 1,), dtype=jnp.float32) * 0.02
        scale = jnp.asarray(1.0 / np.sqrt(C), dtype=jnp.float32)
        return {'x': x, 'ln1_g': ln1_g, 'ln1_b': ln1_b, 'qkv_w': qkv_w, 'qkv_b': qkv_b, 'bias_table': bias_table, 'scale': scale, 'proj_w': proj_w, 'proj_b': proj_b, 'ln2_g': ln2_g, 'ln2_b': ln2_b}
    _L0_attn_all = _L0_attn_setup()
    _L0_attn_in = {k: v for k, v in _L0_attn_all.items() if k in ('ln1_g', 'ln1_b', 'qkv_w', 'qkv_b', 'bias_table', 'scale', 'proj_w', 'proj_b', 'ln2_g', 'ln2_b')}
    del _L0_attn_all

    def _L0_ffn_setup():
        import jax, jax.numpy as jnp
        import numpy as np
        D_MODEL = 64
        N_EXPERTS = 16
        HIDDEN = 128
        SCALE = 0.02
        key = jax.random.key(seed)
        ks = jax.random.split(key, 5)
        x = jax.random.normal(ks[0], (4, 2048, D_MODEL), dtype=jnp.float32)
        gate_w = jax.random.normal(ks[1], (D_MODEL, N_EXPERTS), dtype=jnp.float32) * SCALE
        gate_b = jnp.zeros((N_EXPERTS,), dtype=jnp.float32)
        w1 = jax.random.normal(ks[2], (N_EXPERTS, D_MODEL, HIDDEN), dtype=jnp.float32) * SCALE
        w2 = jax.random.normal(ks[3], (N_EXPERTS, D_MODEL, HIDDEN), dtype=jnp.float32) * SCALE
        w3 = jax.random.normal(ks[4], (N_EXPERTS, HIDDEN, D_MODEL), dtype=jnp.float32) * SCALE
        return {'x': x, 'gate_w': gate_w, 'gate_b': gate_b, 'w1': w1, 'w2': w2, 'w3': w3}
    _L0_ffn_all = _L0_ffn_setup()
    _L0_ffn_in = {k: v for k, v in _L0_ffn_all.items() if k in ('gate_w', 'gate_b', 'w1', 'w2', 'w3')}
    del _L0_ffn_all
    return {'x': x, 'L0_tok_weight': _L0_tok_in['weight'], 'L0_tok_bias': _L0_tok_in['bias'], 'L0_attn_ln1_g': _L0_attn_in['ln1_g'], 'L0_attn_ln1_b': _L0_attn_in['ln1_b'], 'L0_attn_qkv_w': _L0_attn_in['qkv_w'], 'L0_attn_qkv_b': _L0_attn_in['qkv_b'], 'L0_attn_bias_table': _L0_attn_in['bias_table'], 'L0_attn_scale': _L0_attn_in['scale'], 'L0_attn_proj_w': _L0_attn_in['proj_w'], 'L0_attn_proj_b': _L0_attn_in['proj_b'], 'L0_attn_ln2_g': _L0_attn_in['ln2_g'], 'L0_attn_ln2_b': _L0_attn_in['ln2_b'], 'L0_ffn_gate_w': _L0_ffn_in['gate_w'], 'L0_ffn_gate_b': _L0_ffn_in['gate_b'], 'L0_ffn_w1': _L0_ffn_in['w1'], 'L0_ffn_w2': _L0_ffn_in['w2'], 'L0_ffn_w3': _L0_ffn_in['w3']}

def reference(x, L0_tok_weight, L0_tok_bias, L0_attn_ln1_g, L0_attn_ln1_b, L0_attn_qkv_w, L0_attn_qkv_b, L0_attn_bias_table, L0_attn_scale, L0_attn_proj_w, L0_attn_proj_b, L0_attn_ln2_g, L0_attn_ln2_b, L0_ffn_gate_w, L0_ffn_gate_b, L0_ffn_w1, L0_ffn_w2, L0_ffn_w3):
    import jax
    import jax.numpy as jnp

    def _L0_tok_ref(x, weight, bias):
        import jax, jax.numpy as jnp
        import numpy as np
        PH, PW = (64, 25)
        SH, SW = (64, 12)

        def _unfold(x, ph, pw, sh, sw):
            B, C, H, W = x.shape
            nh = (H - ph) // sh + 1
            nw = (W - pw) // sw + 1
            rows = jnp.arange(nh)[:, None] * sh + jnp.arange(ph)[None, :]
            cols = jnp.arange(nw)[:, None] * sw + jnp.arange(pw)[None, :]
            p = x[:, :, rows, :]
            p = p[:, :, :, :, cols]
            p = jnp.transpose(p, (0, 2, 4, 1, 3, 5))
            return p.reshape(B, nh * nw, C * ph * pw)
        p = _unfold(x, PH, PW, SH, SW)
        return jax.nn.gelu(jnp.einsum('bnk,kd->bnd', p, weight) + bias, approximate=False)

    def _L0_attn_ref(x, ln1_g, ln1_b, qkv_w, qkv_b, bias_table, scale, proj_w, proj_b, ln2_g, ln2_b):
        import jax, jax.numpy as jnp
        import numpy as np
        SEQ_LEN = 512
        EMBED_DIM = 64
        BATCH = 8
        LN_EPS = 1e-05

        def _layernorm(x, g, b):
            mu = jnp.mean(x, axis=-1, keepdims=True)
            var = jnp.mean(jnp.square(x - mu), axis=-1, keepdims=True)
            return (x - mu) * jax.lax.rsqrt(var + LN_EPS) * g + b
        B, N, C = x.shape
        h = _layernorm(x, ln1_g, ln1_b)
        qkv = h @ qkv_w + qkv_b
        q, k, v = jnp.split(qkv, 3, axis=-1)
        coords = jnp.arange(N)
        rel_idx = coords[None, :] - coords[:, None] + (N - 1)
        rel_bias = bias_table[rel_idx]
        attn = jnp.einsum('bnc,bmc->bnm', q, k) + rel_bias
        attn = jax.nn.softmax(attn, axis=-1) * scale
        out = jnp.einsum('bnm,bmc->bnc', attn, v)
        out = out @ proj_w + proj_b
        out = _layernorm(out, ln2_g, ln2_b)
        return out

    def _L0_ffn_ref(x, gate_w, gate_b, w1, w2, w3):
        import jax, jax.numpy as jnp
        import numpy as np
        D_MODEL = 64
        N_EXPERTS = 16
        HIDDEN = 128
        SCALE = 0.02
        n_experts = w1.shape[0]
        logits = jnp.einsum('bsd,de->bse', x, gate_w) + gate_b
        probs = jax.nn.softmax(logits, axis=-1)
        top_probs, top_idx = jax.lax.top_k(probs, 2)
        top_probs = top_probs / jnp.sum(top_probs, axis=-1, keepdims=True)
        dispatch = jnp.sum(jax.nn.one_hot(top_idx, n_experts, dtype=x.dtype) * top_probs[..., None], axis=-2)
        h1 = jnp.einsum('bsd,edh->bseh', x, w1)
        h2 = jnp.einsum('bsd,edh->bseh', x, w2)
        hidden = jax.nn.silu(h1) * h2
        expert_out = jnp.einsum('bseh,eho->bseo', hidden, w3)
        return jnp.einsum('bseo,bse->bso', expert_out, dispatch)
    h = _L0_tok_ref(x, L0_tok_weight, L0_tok_bias)
    h = h + _L0_attn_ref(_layernorm(h, axis=-1), L0_attn_ln1_g, L0_attn_ln1_b, L0_attn_qkv_w, L0_attn_qkv_b, L0_attn_bias_table, L0_attn_scale, L0_attn_proj_w, L0_attn_proj_b, L0_attn_ln2_g, L0_attn_ln2_b)
    h = h + _L0_ffn_ref(_layernorm(h, axis=-1), L0_ffn_gate_w, L0_ffn_gate_b, L0_ffn_w1, L0_ffn_w2, L0_ffn_w3)
    return h

_drawn_inputs = setup_inputs


def setup_inputs(seed=0):
    import zlib

    import numpy as np

    out = dict(_drawn_inputs(seed))
    spreads = {'L0_tok_bias': (0.0, 0.1),
     'L0_attn_ln1_g': (1.0, 0.6),
     'L0_attn_ln1_b': (0.0, 0.8),
     'L0_attn_qkv_b': (0.0, 0.455),
     'L0_attn_proj_b': (0.0, 0.1),
     'L0_attn_ln2_g': (1.0, 0.2),
     'L0_attn_ln2_b': (0.0, 0.1),
     'L0_ffn_gate_b': (0.0, 0.8)}
    factors = {'L0_attn_qkv_w': 4.601,
     'L0_attn_bias_table': 8.0,
     'L0_attn_proj_w': 2.842,
     'L0_ffn_gate_w': 8.0,
     'L0_ffn_w1': 8.0,
     'L0_ffn_w2': 8.0,
     'L0_ffn_w3': 8.0}
    for name, (base, spread) in spreads.items():
        noise = np.random.default_rng([zlib.crc32(name.encode()), seed]).standard_normal(out[name].shape)
        drawn = base * np.exp(spread * noise) if base else spread * noise
        out[name] = jnp.asarray(drawn.astype(out[name].dtype))
    for name, factor in factors.items():
        out[name] = (out[name] * factor).astype(out[name].dtype)
    return out
```

```python
from contextlib import ExitStack

import concourse.bass as bass
from concourse import mybir

ALU = mybir.AluOpType
ACT = mybir.ActivationFunctionType
F32 = mybir.dt.float32
F32R = mybir.dt.float32r
U32 = mybir.dt.uint32
AX_X = mybir.AxisListType.X

IMAGES, SIDE = 64, 96
PH, PW, STRIDE = 64, 25, 12
SEQ = (SIDE - PW) // STRIDE + 1
C = 64
COLS = STRIDE * (SEQ - 1) + PW
HCOLS = (COLS + 1) // 2
HSTEP = STRIDE // 2
TAPS = (PW + 1) // 2

TILE_IMAGES = 16
TOK = TILE_IMAGES * SEQ
TILES = IMAGES // TILE_IMAGES
CHUNK = 2
CHUNKS = TILES // CHUNK
CTOK = CHUNK * TOK
ALL = TILES * TOK
MASKED = -1.0e30

EXPERTS, HIDDEN, TOP = 16, 128, 2
GROUP = 4
EPS = 1e-5
FFN_COLS = 2 * GROUP * HIDDEN + GROUP * C
WARM = 14

SMALL, SMALL_COLS = {}, 0
for _name, _rows, _n in (("tokb", 128, 1), ("ln1_b", C, 1), ("ln1_g", C, 1), ("scale", TOK, 1), ("qkv", C + 1, 3 * C),
                         ("proj", C + 1, C), ("ln2_g", C + 1, C), ("ln2_b", TOK, C), ("rel", TOK, SEQ),
                         ("gate_w", 128, EXPERTS), ("gate_b", 1, EXPERTS)):
    SMALL[_name] = (_rows, SMALL_COLS, _n)
    SMALL_COLS += _n


def vit_tower(nc, img_in, tokw_in, small_in, ffn_in, out):
    with ExitStack() as ctx:
        def sb(name, shape, dt=F32):
            return ctx.enter_context(nc.sbuf_tensor(name, shape, dt))

        def bank(name):
            return ctx.enter_context(nc.psum_tensor(name, [128, 512], F32))

        def sem(name):
            return ctx.enter_context(nc.semaphore(name))

        ps_a = [bank(f"ps_a{c}") for c in range(CHUNKS)]
        ps_b = [bank(f"ps_b{c}") for c in range(CHUNKS)]
        ps_c = [bank(f"ps_c{c}") for c in range(CHUNKS)]
        ps_p = bank("ps_p")
        ps_d = bank("ps_d")

        img = sb("img", [128, IMAGES, HCOLS])
        tokw = sb("tokw", [128, TAPS, C])
        small = sb("small", [128, SMALL_COLS])
        warm = sb("warm", [128, 512], mybir.dt.bfloat16)
        ident = sb("ident", [128, 128])
        fold2 = sb("fold2", [128, C])
        half_neg = sb("half_neg", [128, TILES])
        lnL = sb("lnL", [C + 1, C + 1])
        wT = sb("wT", [C, 3, C + 1])
        G = sb("G", [C + 1, C + 1])
        projm = sb("projm", [C + 1, 1])
        projX = sb("projX", [C + 1, 2 * C])
        VW = sb("VW", [C + 1, 2 * C])
        relmask = sb("relmask", [TOK, TOK])
        ones_row = sb("ones_row", [1, TOK])
        iota16 = sb("iota16", [TOK, EXPERTS])
        sel = sb("sel", [2 * EXPERTS, EXPERTS])
        selr = sb("selr", [2 * EXPERTS, EXPERTS, C], F32R)

        gT = sb("gT", [128, CHUNKS, TOK])
        h0b = sb("h0b", [TOK, TILES, C])
        y = sb("y", [TOK, TILES, C])
        yT = sb("yT", [C + 1, ALL])
        Z = sb("Z", [C + 1, ALL])
        V = sb("V", [TOK, TILES, 2 * C])
        P = sb("P", [TOK, TILES, TOK])
        PT = sb("PT", [TOK, TILES, TOK])
        h1 = sb("h1", [TOK, TILES, C])
        x3 = sb("x3", [TOK, TILES, 2, C])
        xs = sb("xs", [128, ALL], F32R)
        stats = sb("stats", [TOK, 3, TILES, 6])
        mv = sb("mv", [TOK, 3, TILES, 2])
        ve = sb("ve", [TOK, 3, TILES])
        rstd = sb("rstd", [TOK, 3, TILES])
        nmax = sb("nmax", [TOK, TILES])
        psum_ = sb("psum_", [TOK, TILES])
        prec = sb("prec", [TOK, TILES])

        top8 = sb("top8", [TOK, TILES, 8])
        idx8 = sb("idx8", [TOK, TILES, 8], U32)
        gap = sb("gap", [TOK, TILES])
        tnh = sb("tnh", [TOK, TILES])
        wtop = sb("wtop", [TOK, TILES, TOP])
        hot = sb("hot", [TOK, TILES, TOP, EXPERTS])
        disp = sb("disp", [TOK, TILES, EXPERTS])
        dsp = sb("dsp", [TOK, TILES, 2, EXPERTS])
        dspr = sb("dspr", [TOK, TILES, EXPERTS], F32R)
        dT = sb("dT", [2 * EXPERTS, ALL], F32R)
        D = sb("D", [128, 2, ALL])

        ffn = sb("ffn", [128, EXPERTS // GROUP, FFN_COLS])
        whi = sb("whi", [128, 2, EXPERTS, HIDDEN], F32R)
        wlo = sb("wlo", [128, 2, EXPERTS, HIDDEN], F32R)
        sil = sb("sil", [HIDDEN, 4, ALL])
        hid = sb("hid", [HIDDEN, 4, ALL])
        prod = sb("prod", [128, 4, ALL])
        acc = sb("acc", [128, 2, ALL])
        res = sb("res", [TOK, TILES, C])

        def part(name):
            rows, c0, n = SMALL[name]
            return small[0:rows, c0:c0 + n]

        tokb, lnb, g1col, qkvR, projR, g2row, b2row, scale_c, rel_rows, gate_w2, gate_row = (
            part(n) for n in ("tokb", "ln1_b", "ln1_g", "qkv", "proj", "ln2_g", "ln2_b", "scale", "rel",
                              "gate_w", "gate_b"))

        def raw12(e):
            return ffn[:, e // GROUP, 0:2 * GROUP * HIDDEN].rearrange(
                "p (i e h) -> p i e h", i=2, e=GROUP)[:, :, e % GROUP, :]

        def w3_of(e):
            c0 = 2 * GROUP * HIDDEN + (e % GROUP) * C
            return ffn[:, e // GROUP, c0:c0 + C]

        s_tokw, s_small, s_out = sem("s_tokw"), sem("s_small"), sem("s_out")
        s_img = [sem(f"s_img{t}") for t in range(TILES)]
        s_ffn = [sem(f"s_ffn{g}") for g in range(EXPERTS // GROUP)]
        warm_ready = sem("warm_ready")
        pool_const = sem("pool_const")
        ident_ready = sem("ident_ready")
        mask_ready = sem("mask_ready")
        sel_ready = sem("sel_ready")
        half_ready = sem("half_ready")
        ones_ready = sem("ones_ready")
        fold_ready = sem("fold_ready")
        lnL_ready = sem("lnL_ready")
        projX_ready = sem("projX_ready")
        wT_psum, wT_ready = sem("wT_psum"), sem("wT_ready")
        GV_psum, GV_ready = sem("GV_psum"), sem("GV_ready")
        conv_done, gelu_done, h0_done = sem("conv_done"), sem("gelu_done"), sem("h0_done")
        ve_ready, rstd_ready = sem("ve_ready"), sem("rstd_ready")
        y_ready, yT_psum, yT_ready = sem("y_ready"), sem("yT_psum"), sem("yT_ready")
        Z_psum, Z_ready, V_psum, V_ready = sem("Z_psum"), sem("Z_ready"), sem("V_psum"), sem("V_ready")
        score_done, max_ready, exp_done = sem("score_done"), sem("max_ready"), sem("exp_done")
        P_ready, PT_psum, PT_ready = sem("P_ready"), sem("PT_psum"), sem("PT_ready")
        attn_done, h1_ready, x3_ready = sem("attn_done"), sem("h1_ready"), sem("x3_ready")
        xT_psum, xs_lower, xs_upper = sem("xT_psum"), sem("xs_lower"), sem("xs_upper")
        logit_done, gap_ready, tanh_done = sem("logit_done"), sem("gap_ready"), sem("tanh_done")
        disp_ready, dT_psum, dT_ready = sem("disp_ready"), sem("dT_psum"), sem("dT_ready")
        D_psum, D_ready = sem("D_psum"), sem("D_ready")
        whi_ready, wlo_ready = sem("whi_ready"), sem("wlo_ready")
        up1_done, up2_done, silu_done, hid_ready = sem("up1_done"), sem("up2_done"), sem("silu_done"), sem("hid_ready")
        down_done, prod_ready, acc_done = sem("down_done"), sem("prod_ready"), sem("acc_done")
        res_psum, res_ready = sem("res_psum"), sem("res_ready")
        dve_step = sem("dve_step")
        pool_step = sem("pool_step")

        out_dst = out.rearrange("(t i) n d -> (i n) t d", t=TILES)

        block = ctx.enter_context(nc.Block())

        @block.sync
        def _(sp):
            sp.dma_start(tokw[:], tokw_in).then_inc(s_tokw, 16)
            for t in range(TILES):
                b = slice(t * TILE_IMAGES, (t + 1) * TILE_IMAGES)
                sp.dma_start(img[:, b, :], img_in[t]).then_inc(s_img[t], 16)
            for g in range(EXPERTS // GROUP):
                sp.dma_start(ffn[:, g, :], ffn_in[g]).then_inc(s_ffn[g], 16)
            sp.wait_ge(res_ready, 1)
            sp.dma_start(out_dst, res[:]).then_inc(s_out, 16)
            sp.wait_ge(s_out, 16)

        @block.gpsimd
        def _(pool):
            n_step = [0]

            def link(ins):
                n_step[0] += 1
                ins.then_inc(pool_step, 1)
                pool.wait_ge(pool_step, n_step[0])

            nc.gpsimd.memset(half_neg[:], -0.5).then_inc(half_ready, 1)
            link(nc.gpsimd.memset(ident[:], 0.0))
            nc.gpsimd.affine_select(out=ident[:], in_=ident[:], compare_op=ALU.not_equal, fill=1.0, base=0,
                                    pattern=[[-1, 128]], channel_multiplier=1).then_inc(ident_ready, 1)
            nc.gpsimd.memset(ones_row[:], 1.0).then_inc(ones_ready, 1)
            pool.wait_ge(s_small, 16)
            rel_b = rel_rows.rearrange("p (a j) -> p a j", a=1).to_broadcast([TOK, TILE_IMAGES, SEQ])
            mask3 = relmask[:].rearrange("p (b j) -> p b j", j=SEQ)
            link(nc.gpsimd.affine_select(out=mask3, in_=rel_b, compare_op=ALU.is_ge, fill=MASKED, base=0,
                                         pattern=[[-SEQ, TILE_IMAGES], [0, SEQ]], channel_multiplier=1))
            nc.gpsimd.affine_select(out=mask3, in_=mask3, compare_op=ALU.is_ge, fill=MASKED, base=SEQ - 1,
                                    pattern=[[SEQ, TILE_IMAGES], [0, SEQ]], channel_multiplier=-1
                                    ).then_inc(mask_ready, 1)
            nc.gpsimd.iota(iota16[:], pattern=[[1, EXPERTS]], base=0, channel_multiplier=0,
                           allow_small_or_imprecise_dtypes=True).then_inc(pool_const, 1)

            def low_part(e):
                pool.wait_ge(whi_ready, e + 1)
                nc.gpsimd.tensor_tensor(wlo[:, :, e, :], raw12(e), whi[:, :, e, :].bitcast(F32),
                                        ALU.subtract).then_inc(wlo_ready, 1)

            def power(k, c, n):
                pool.wait_ge(ve_ready, n)
                t = slice(c * CHUNK, (c + 1) * CHUNK)
                nc.gpsimd.tensor_tensor(rstd[:, k, t], ve[:, k, t], half_neg[0:TOK, t],
                                        ALU.pow).then_inc(rstd_ready, 1)

            for n, (k, c) in enumerate(LN_ORDER):
                power(k, c, n + 1)
            for e in range(4):
                low_part(e)
            for e in range(4, EXPERTS):
                low_part(e)
                if e % 2 == 1 and e >= 9:
                    add_pair(nc, pool, (e - 9) // 2 + 1, prod, acc, prod_ready, acc_done)
            for p in range(4 + 1, EXPERTS // 2):
                add_pair(nc, pool, p, prod, acc, prod_ready, acc_done)

        @block.scalar
        def _(act):
            act.dma_start(small[:], small_in).then_inc(s_small, 16)
            nc.scalar.preload_act_table(ACT.Gelu)
            act.wait_ge(s_small, 16)
            for c in range(CHUNKS):
                act.wait_ge(conv_done, c + 1)
                nc.scalar.activation(gT[:, c, :], ps_a[c][:, 0:TOK], ACT.Gelu, bias=tokb
                                     ).then_inc(gelu_done, 1)
            nc.scalar.preload_act_table(ACT.Exp)
            for c in range(CHUNKS):
                t0 = c * CHUNK
                act.wait_ge(V_psum, c + 1)
                nc.scalar.copy(V[:, t0:t0 + CHUNK, :], ps_b[c][0:TOK, 0:CHUNK * 2 * C].rearrange(
                    "p (t n) -> p t n", t=CHUNK)).then_inc(V_ready, 1)
                act.wait_ge(max_ready, c + 1)
                for t in range(CHUNK):
                    nc.scalar.activation(P[:, t0 + t, :], ps_c[c][0:TOK, t * TOK:(t + 1) * TOK], ACT.Exp,
                                         bias=nmax[:, t0 + t:t0 + t + 1],
                                         accum_out=psum_[:, t0 + t:t0 + t + 1]).then_inc(exp_done, 1)
            def round_weights(e):
                act.wait_ge(s_ffn[e // GROUP], 16)
                nc.scalar.copy(whi[:, :, e, :], raw12(e)).then_inc(whi_ready, 1)

            for e in range(4):
                round_weights(e)
            for c in range(CHUNKS):
                act.wait_ge(xT_psum, c + 1)
                nc.scalar.copy(xs[0:C, c * CTOK:(c + 1) * CTOK], ps_b[c][0:C, 0:CTOK]).then_inc(xs_lower, 1)
            act.wait_ge(gap_ready, 1)
            nc.scalar.activation(tnh[:], gap[:], ACT.Tanh, scale=0.5).then_inc(tanh_done, 1)
            nc.scalar.preload_act_table(ACT.Silu)

            def spread(p):
                act.wait_ge(D_psum, p + 1)
                if p >= 2:
                    act.wait_ge(prod_ready, p - 1)
                nc.scalar.copy(D[:, p % 2, :], ps_d[:, 0:ALL]).then_inc(D_ready, 1)

            for e in range(EXPERTS):
                act.wait_ge(up1_done, e + 1)
                if e >= 4:
                    act.wait_ge(hid_ready, e - 3)
                nc.scalar.activation(sil[:, e % 4, :], ps_c[e % 2][:, 0:ALL], ACT.Silu).then_inc(silu_done, 1)
                if e + 4 < EXPERTS:
                    round_weights(e + 4)
                if e % 2 == 1 and e >= 3:
                    spread((e - 3) // 2)
            spread(EXPERTS // 2 - 1)

        @block.vector
        def _(dve):
            n_step = [0]

            def link(*instructions):
                for ins in instructions:
                    n_step[0] += 1
                    ins.then_inc(dve_step, 1)
                dve.wait_ge(dve_step, n_step[0])

            nc.vector.memset(warm[:], 0.0).then_inc(warm_ready, 1)
            nc.vector.memset(lnL[C:C + 1, 0:C], 0.0).then_inc(lnL_ready, 1)
            nc.vector.memset(lnL[C:C + 1, C:C + 1], 1.0).then_inc(lnL_ready, 1)
            nc.vector.memset(yT[C:C + 1, :], 1.0).then_inc(lnL_ready, 1)
            dve.wait_ge(ident_ready, 1)
            nc.vector.tensor_tensor(fold2[:], ident[:, 0:C], ident[:, C:128], ALU.add).then_inc(fold_ready, 1)
            dve.wait_ge(s_small, 16)
            nc.vector.tensor_copy(lnL[0:C, C:C + 1], lnb).then_inc(lnL_ready, 1)
            nc.vector.tensor_scalar(lnL[0:C, 0:C], ident[0:C, 0:C], g1col, None, ALU.mult
                                    ).then_inc(lnL_ready, 1)
            link(nc.vector.tensor_reduce(projm[:], projR, AX_X, ALU.add))
            link(nc.vector.tensor_scalar(projm[:], projm[:], 1.0 / C, None, ALU.mult))
            link(nc.vector.tensor_scalar(projX[:, 0:C], projR, projm[:, 0:1], None, ALU.subtract))
            nc.vector.tensor_tensor(projX[:, C:2 * C], projX[:, 0:C], g2row, ALU.mult).then_inc(projX_ready, 1)
            dve.wait_ge(wT_psum, 1)
            nc.vector.tensor_copy(wT[:], ps_p[0:C, 0:3 * (C + 1)].rearrange("p (i n) -> p i n", i=3)
                                  ).then_inc(wT_ready, 1)
            dve.wait_ge(GV_psum, 1)
            nc.vector.tensor_copy(G[:], ps_d[0:C + 1, 0:C + 1]).then_inc(GV_ready, 1)
            nc.vector.tensor_copy(VW[:], ps_d[0:C + 1, 128:128 + 2 * C]).then_inc(GV_ready, 1)
            link(nc.vector.tensor_tensor(sel[:], ident[0:2 * EXPERTS, 0:EXPERTS],
                                         ident[0:2 * EXPERTS, EXPERTS:2 * EXPERTS], ALU.add))
            nc.vector.tensor_copy(selr[:], sel[:].rearrange("p (e a) -> p e a", a=1).to_broadcast(
                [2 * EXPERTS, EXPERTS, C])).then_inc(fold_ready, 1)

            def normal_stats(k, c, sources, mul, add):
                t0 = c * CHUNK
                link(*[nc.vector.bn_stats(stats[:, k, t0 + t, :], sources[t]) for t in range(CHUNK)])
                link(*[nc.vector.bn_aggr(mv[:, k, t0 + t, :], stats[:, k, t0 + t, :]) for t in range(CHUNK)])
                nc.vector.tensor_scalar(ve[:, k, t0:t0 + CHUNK], mv[:, k, t0:t0 + CHUNK, 1], mul, add,
                                        ALU.mult, ALU.add).then_inc(ve_ready, 1)

            def norm_in(c):
                t0 = c * CHUNK
                dve.wait_ge(h0_done, c + 1)
                h0 = [ps_a[c][0:TOK, 128 + t * C:128 + (t + 1) * C] for t in range(CHUNK)]
                normal_stats(0, c, h0, 1.0 + EPS, EPS * EPS)
                link(*[nc.vector.tensor_tensor(h0b[:, t0 + t, :], h0[t], b2row, ALU.add) for t in range(CHUNK)])
                dve.wait_ge(rstd_ready, LN_ORDER.index((0, c)) + 1)
                for t in range(CHUNK):
                    nc.vector.tensor_scalar(y[:, t0 + t, :], h0[t], mv[:, 0, t0 + t, 0:1], rstd[:, 0, t0 + t:t0 + t + 1],
                                            ALU.subtract, ALU.mult).then_inc(y_ready, 1)
                dve.wait_ge(yT_psum, c + 1)
                nc.vector.tensor_copy(yT[0:C, c * CTOK:(c + 1) * CTOK], ps_a[c][0:C, 256:256 + CTOK]
                                      ).then_inc(yT_ready, 1)
                dve.wait_ge(Z_psum, c + 1)
                nc.vector.tensor_copy(Z[:, c * CTOK:(c + 1) * CTOK], ps_a[c][0:C + 1, 0:CTOK]).then_inc(Z_ready, 1)

            def softmax(c):
                t0 = c * CHUNK
                dve.wait_ge(score_done, c + 1)
                nc.vector.tensor_reduce(nmax[:, t0:t0 + CHUNK],
                                        ps_c[c][0:TOK, 0:CTOK].rearrange("p (t m) -> p t m", t=CHUNK),
                                        AX_X, ALU.max, negate=True).then_inc(max_ready, 1)
                dve.wait_ge(exp_done, CHUNK * (c + 1))
                link(nc.vector.reciprocal(prec[:, t0:t0 + CHUNK], psum_[:, t0:t0 + CHUNK]))
                for t in range(CHUNK):
                    nc.vector.tensor_scalar(P[:, t0 + t, :], P[:, t0 + t, :], prec[:, t0 + t:t0 + t + 1],
                                            scale_c, ALU.mult, ALU.mult).then_inc(P_ready, 1)
                dve.wait_ge(PT_psum, c + 1)
                nc.vector.tensor_copy(PT[:, t0:t0 + CHUNK, :], ps_b[c][0:TOK, 0:CTOK].rearrange(
                    "p (t m) -> p t m", t=CHUNK)).then_inc(PT_ready, 1)

            def norm_out(c):
                t0 = c * CHUNK
                dve.wait_ge(attn_done, c + 1)
                a = [ps_a[c][0:TOK, t * 2 * C:t * 2 * C + 2 * C] for t in range(CHUNK)]
                normal_stats(1, c, [v[:, 0:C] for v in a], 1.0, EPS)
                dve.wait_ge(rstd_ready, LN_ORDER.index((1, c)) + 1)
                link(*[nc.vector.scalar_tensor_tensor(h1[:, t0 + t, :], a[t][:, C:2 * C],
                                                      rstd[:, 1, t0 + t:t0 + t + 1], h0b[:, t0 + t, :],
                                                      ALU.mult, ALU.add) for t in range(CHUNK)])
                normal_stats(2, c, [h1[:, t0 + t, :] for t in range(CHUNK)], 1.0, EPS)
                dve.wait_ge(rstd_ready, LN_ORDER.index((2, c)) + 1)
                for t in range(CHUNK):
                    twice = h1[:, t0 + t:t0 + t + 1, :].to_broadcast([TOK, 2, C])
                    nc.vector.tensor_scalar(x3[:, t0 + t, :, :], twice, mv[:, 2, t0 + t, 0:1],
                                            rstd[:, 2, t0 + t:t0 + t + 1], ALU.subtract, ALU.mult
                                            ).then_inc(x3_ready, 1)

            def split_x(c):
                cols = slice(c * CTOK, (c + 1) * CTOK)
                dve.wait_ge(xT_psum, c + 1)
                link(nc.vector.tensor_copy(xs[C:128, cols], ps_b[c][C:128, 0:CTOK]))
                nc.vector.tensor_tensor(xs[C:128, cols], ps_b[c][C:128, 0:CTOK], xs[C:128, cols].bitcast(F32),
                                        ALU.subtract).then_inc(xs_upper, 1)

            norm_in(0)
            softmax(0)
            norm_in(1)
            norm_out(0)
            softmax(1)
            split_x(0)
            norm_out(1)
            split_x(1)

            dve.wait_ge(logit_done, 1)
            lg = ps_p[0:TOK, 0:TILES * EXPERTS].rearrange("p (t e) -> p t e", t=TILES)
            link(*[nc.vector.max(top8[:, t, :], lg[:, t, :]) for t in range(TILES)])
            nc.vector.tensor_tensor(gap[:], top8[:, :, 0], top8[:, :, 1], ALU.subtract).then_inc(gap_ready, 1)
            link(*[nc.vector.max_index(idx8[:, t, :], top8[:, t, :], lg[:, t, :]) for t in range(TILES)])
            dve.wait_ge(pool_const, 1)
            for k in range(TOP):
                link(nc.vector.tensor_tensor(
                    hot[:, :, k, :],
                    iota16[:].rearrange("p (a e) -> p a e", a=1).to_broadcast([TOK, TILES, EXPERTS]),
                    idx8[:, :, k:k + 1].to_broadcast([TOK, TILES, EXPERTS]), ALU.is_equal))
            dve.wait_ge(tanh_done, 1)
            link(nc.vector.tensor_scalar(wtop[:, :, 0], tnh[:], 0.5, 0.5, ALU.mult, ALU.add),
                 nc.vector.tensor_scalar(wtop[:, :, 1], tnh[:], -0.5, 0.5, ALU.mult, ALU.add))
            link(*[nc.vector.tensor_tensor(hot[:, :, k, :], hot[:, :, k, :],
                                           wtop[:, :, k:k + 1].to_broadcast([TOK, TILES, EXPERTS]), ALU.mult)
                   for k in range(TOP)])
            link(nc.vector.tensor_tensor(disp[:], hot[:, :, 0, :], hot[:, :, 1, :], ALU.add))
            link(nc.vector.tensor_copy(dspr[:], disp[:]))
            nc.vector.tensor_copy(dsp[:, :, 0, :], dspr[:].bitcast(F32)).then_inc(disp_ready, 1)
            nc.vector.tensor_tensor(dsp[:, :, 1, :], disp[:], dspr[:].bitcast(F32), ALU.subtract
                                    ).then_inc(disp_ready, 1)

            def hidden(e):
                dve.wait_ge(silu_done, e + 1)
                dve.wait_ge(up2_done, e + 1)
                if e >= 4:
                    dve.wait_ge(down_done, e // 2 - 1)
                nc.vector.tensor_tensor(hid[:, e % 4, :], ps_a[e % 2][:, 0:ALL], sil[:, e % 4, :], ALU.mult
                                        ).then_inc(hid_ready, 1)

            def weigh(p):
                dve.wait_ge(down_done, p + 1)
                dve.wait_ge(D_ready, p + 1)
                if p >= 4:
                    dve.wait_ge(acc_done, p - 3 if p > 4 else 1)
                nc.vector.tensor_tensor(prod[:, p % 4, :], ps_b[p % 2][:, 0:ALL], D[:, p % 2, :], ALU.mult
                                        ).then_inc(prod_ready, 1)

            hidden(0)
            hidden(1)
            dve.wait_ge(dT_psum, 1)
            nc.vector.tensor_copy(dT[:], ps_p[0:2 * EXPERTS, 0:ALL]).then_inc(dT_ready, 1)
            for e in range(2, EXPERTS):
                hidden(e)
                if e % 2 == 1:
                    weigh((e - 3) // 2)
            weigh(EXPERTS // 2 - 1)
            dve.wait_ge(res_psum, 1)
            nc.vector.tensor_tensor(res[:], ps_p[0:TOK, 0:TILES * C].rearrange("p (t d) -> p t d", t=TILES),
                                    h1[:], ALU.add).then_inc(res_ready, 1)

        @block.tensor
        def _(pe):
            mm = nc.tensor.matmul

            pe.wait_ge(warm_ready, 1)
            for i in range(WARM):
                mm(ps_b[1][:], warm[:, 0:128], warm[:], start=True, stop=True)
            pe.wait_ge(lnL_ready, 5)
            for i in range(3):
                last = mm(ps_p[0:C, i * (C + 1):(i + 1) * (C + 1)], qkvR[:, i * C:(i + 1) * C], lnL[:],
                          start=True, stop=True)
            last.then_inc(wT_psum, 1)
            pe.wait_ge(wT_ready, 1)
            pe.wait_ge(projX_ready, 1)
            mm(ps_d[0:C + 1, 0:C + 1], wT[:, 0, :], wT[:, 1, :], start=True, stop=True)
            mm(ps_d[0:C + 1, 128:128 + 2 * C], wT[:, 2, :], projX[0:C, :], start=True, stop=True
               ).then_inc(GV_psum, 1)
            pe.wait_ge(mask_ready, 1)
            for c in range(CHUNKS):
                two = relmask[:].rearrange("p (a m) -> p a m", a=1).to_broadcast([TOK, CHUNK, TOK])
                mm(ps_c[c][0:TOK, 0:CTOK].rearrange("p (t m) -> p t m", t=CHUNK), ident[0:TOK, 0:TOK], two,
                   start=True, stop=False, skip_group_check=True)

            def conv(c):
                for t in range(CHUNK):
                    tt = c * CHUNK + t
                    pe.wait_ge(s_img[tt], 16)
                last = None
                for j in range(TAPS):
                    k = 128 if j < TAPS - 1 else C
                    for t in range(CHUNK):
                        b0 = (c * CHUNK + t) * TILE_IMAGES
                        patch = img[0:k, b0:b0 + TILE_IMAGES, j:j + HSTEP * (SEQ - 1) + 1:HSTEP]
                        last = mm(ps_a[c][t * C:(t + 1) * C, 0:TOK].rearrange("p (b n) -> p b n", n=SEQ),
                                  tokw[0:k, j, :], patch, start=(j == 0), stop=(j == TAPS - 1))
                last.then_inc(conv_done, 1)

            def to_tokens(c):
                pe.wait_ge(gelu_done, c + 1)
                nc.tensor.transpose(ps_a[c][0:TOK, 128:256], gT[:, c, :], ident[:]).then_inc(h0_done, 1)

            def y_to_T(c):
                pe.wait_ge(y_ready, CHUNK * (c + 1))
                for t in range(CHUNK):
                    last = nc.tensor.transpose(ps_a[c][0:C, 256 + t * TOK:256 + (t + 1) * TOK],
                                               y[:, c * CHUNK + t, :], ident[0:TOK, 0:TOK])
                last.then_inc(yT_psum, 1)

            def project(c):
                cols = slice(c * CTOK, (c + 1) * CTOK)
                pe.wait_ge(yT_ready, c + 1)
                mm(ps_a[c][0:C + 1, 0:CTOK], G[:], yT[:, cols], start=True, stop=True).then_inc(Z_psum, 1)
                for t in range(CHUNK):
                    tok = slice(c * CTOK + t * TOK, c * CTOK + (t + 1) * TOK)
                    last = mm(ps_b[c][0:TOK, t * 2 * C:(t + 1) * 2 * C], yT[:, tok], VW[:], start=True, stop=True)
                last.then_inc(V_psum, 1)

            def scores(c):
                pe.wait_ge(Z_ready, c + 1)
                for t in range(CHUNK):
                    tok = slice(c * CTOK + t * TOK, c * CTOK + (t + 1) * TOK)
                    last = mm(ps_c[c][0:TOK, t * TOK:(t + 1) * TOK], Z[:, tok], yT[:, tok],
                              start=False, stop=(t == CHUNK - 1), skip_group_check=True)
                last.then_inc(score_done, 1)
                two = projX[C:C + 1, :].rearrange("p (a n) -> p a n", a=1).to_broadcast([1, CHUNK, 2 * C])
                mm(ps_a[c][0:TOK, 0:CHUNK * 2 * C].rearrange("p (t n) -> p t n", t=CHUNK), yT[C:C + 1, 0:TOK], two,
                   start=True, stop=False, skip_group_check=True)

            def attend(c):
                pe.wait_ge(P_ready, CHUNK * (c + 1))
                pe.wait_ge(V_ready, c + 1)
                for t in range(CHUNK):
                    last = nc.tensor.transpose(ps_b[c][0:TOK, t * TOK:(t + 1) * TOK], P[:, c * CHUNK + t, :],
                                               ident[0:TOK, 0:TOK])
                last.then_inc(PT_psum, 1)
                pe.wait_ge(PT_ready, c + 1)
                for t in range(CHUNK):
                    last = mm(ps_a[c][0:TOK, t * 2 * C:(t + 1) * 2 * C], PT[:, c * CHUNK + t, :],
                              V[:, c * CHUNK + t, :], start=False, stop=(t == CHUNK - 1), skip_group_check=True)
                last.then_inc(attn_done, 1)

            def x_to_T(c):
                pe.wait_ge(x3_ready, CHUNK * (c + 1))
                for t in range(CHUNK):
                    last = nc.tensor.transpose(ps_b[c][:, t * TOK:(t + 1) * TOK],
                                               x3[:, c * CHUNK + t, :, :].rearrange("p a d -> p (a d)"),
                                               ident[0:TOK, 0:TOK])
                last.then_inc(xT_psum, 1)

            pe.wait_ge(s_tokw, 16)
            conv(0)
            to_tokens(0)
            y_to_T(0)
            pe.wait_ge(GV_ready, 2)
            project(0)
            scores(0)
            conv(1)
            to_tokens(1)
            attend(0)
            y_to_T(1)
            project(1)
            scores(1)
            x_to_T(0)
            attend(1)
            x_to_T(1)

            pe.wait_ge(ones_ready, 1)
            gate_b4 = gate_row.rearrange("p (a e) -> p a e", a=1).to_broadcast([1, TILES, EXPERTS])
            mm(ps_p[0:TOK, 0:TILES * EXPERTS].rearrange("p (t e) -> p t e", t=TILES), ones_row[:], gate_b4,
               start=True, stop=False, skip_group_check=True)
            pe.wait_ge(xs_lower, CHUNKS)
            pe.wait_ge(xs_upper, CHUNKS)
            for t in range(TILES):
                last = mm(ps_p[0:TOK, t * EXPERTS:(t + 1) * EXPERTS], xs[:, t * TOK:(t + 1) * TOK].bitcast(F32),
                          gate_w2, start=False, stop=(t == TILES - 1), skip_group_check=True)
            last.then_inc(logit_done, 1)

            def up(i, e, dst, done):
                pe.wait_ge(whi_ready, e + 1)
                pe.wait_ge(wlo_ready, e + 1)
                mm(dst[:, 0:ALL], whi[:, i, e, :], xs[:], start=True, stop=False)
                mm(dst[:, 0:ALL], wlo[:, i, e, :], xs[:], start=False, stop=True).then_inc(done, 1)

            def up1(e):
                if e >= 2:
                    pe.wait_ge(silu_done, e - 1)
                up(0, e, ps_c[e % 2], up1_done)

            def up2(e):
                if e >= 2:
                    pe.wait_ge(hid_ready, e - 1)
                up(1, e, ps_a[e % 2], up2_done)

            def down(p):
                if p >= 1:
                    pe.wait_ge(D_ready, p)
                mm(ps_d[:, 0:ALL], selr[:, 2 * p:2 * p + 2, :].rearrange("p a n -> p (a n)"), dT[:],
                   start=True, stop=True).then_inc(D_psum, 1)
                pe.wait_ge(s_ffn[2 * p // GROUP], 16)
                pe.wait_ge(hid_ready, 2 * p + 2)
                if p >= 2:
                    pe.wait_ge(prod_ready, p - 1)
                for h in range(2):
                    e = 2 * p + h
                    last = mm(ps_b[p % 2][h * C:(h + 1) * C, 0:ALL], w3_of(e), hid[:, e % 4, :],
                              start=True, stop=True)
                last.then_inc(down_done, 1)

            up1(0)
            up1(1)
            up2(0)
            up2(1)
            up1(2)
            pe.wait_ge(disp_ready, 2)
            for t in range(TILES):
                last = nc.tensor.transpose(ps_p[0:2 * EXPERTS, t * TOK:(t + 1) * TOK],
                                           dsp[:, t, :, :].rearrange("p s e -> p (s e)"), ident[0:TOK, 0:TOK])
            last.then_inc(dT_psum, 1)
            up1(3)
            pe.wait_ge(dT_ready, 1)
            pe.wait_ge(fold_ready, 2)
            for e in range(2, EXPERTS):
                up2(e)
                if e + 2 < EXPERTS:
                    up1(e + 2)
                if e % 2 == 1:
                    down((e - 3) // 2)
            down(EXPERTS // 2 - 1)
            pe.wait_ge(acc_done, EXPERTS // 2 - 1)
            for t in range(TILES):
                last = mm(ps_p[0:TOK, t * C:(t + 1) * C], acc[:, ACC_LAST, t * TOK:(t + 1) * TOK], fold2[:],
                          start=True, stop=True)
            last.then_inc(res_psum, 1)


LN_ORDER = [(0, 0), (0, 1), (1, 0), (2, 0), (1, 1), (2, 1)]
ACC_LAST = (EXPERTS // 2 - 1) % 2


def add_pair(nc, pool, p, prod, acc, prod_ready, acc_done):
    pool.wait_ge(prod_ready, p + 1)
    if p >= 2:
        pool.wait_ge(acc_done, p - 1)
    before = prod[:, 0, :] if p == 1 else acc[:, (p - 1) % 2, :]
    nc.gpsimd.tensor_tensor(acc[:, p % 2, :], before, prod[:, p % 4, :], ALU.add).then_inc(acc_done, 1)


_OUT = (IMAGES, SEQ, C)


def kernel(**inputs):
    import numpy as np
    from concourse import bacc
    from concourse.bass_utils import run_bass_kernel_spmd

    a = {k.replace("L0_", ""): np.asarray(v) for k, v in inputs.items()}

    def by_parity(v):
        odd = np.concatenate([v[..., 1::2], np.zeros_like(v[..., :1])], axis=-1)
        return v[..., 0::2], odd

    rows = a["x"][:, 0, 0:PH, 0:COLS].reshape(TILES, TILE_IMAGES, PH, COLS).transpose(0, 2, 1, 3)
    img = np.concatenate(by_parity(rows), axis=1)
    taps = a["tok_weight"].reshape(PH, PW, C).transpose(0, 2, 1)
    tokw = np.concatenate(by_parity(taps), axis=0).transpose(0, 2, 1)

    table = a["attn_bias_table"]
    rel = np.stack([table[SEQ - 1 - i:2 * SEQ - 1 - i] for i in range(SEQ)])
    pieces = {
        "tokb": np.tile(a["tok_bias"], 2)[:, None],
        "ln1_b": a["attn_ln1_b"][:, None],
        "ln1_g": a["attn_ln1_g"][:, None],
        "scale": np.broadcast_to(a["attn_scale"], (TOK, 1)),
        "qkv": np.concatenate([a["attn_qkv_w"], a["attn_qkv_b"][None]]),
        "proj": np.concatenate([a["attn_proj_w"], a["attn_proj_b"][None]]),
        "ln2_g": np.broadcast_to(a["attn_ln2_g"], (C + 1, C)),
        "ln2_b": np.broadcast_to(a["attn_ln2_b"], (TOK, C)),
        "rel": np.tile(rel, (TILE_IMAGES, 1)),
        "gate_w": np.tile(a["ffn_gate_w"], (2, 1)),
        "gate_b": a["ffn_gate_b"][None],
    }
    small = np.zeros((128, SMALL_COLS), np.float32)
    for name, (n, c0, cols) in SMALL.items():
        small[0:n, c0:c0 + cols] = pieces[name]

    groups = EXPERTS // GROUP
    up = np.stack([a["ffn_w1"], a["ffn_w2"]]).reshape(2, groups, GROUP, C, HIDDEN).transpose(1, 3, 0, 2, 4)
    up = np.tile(up.reshape(groups, C, 2 * GROUP * HIDDEN), (1, 2, 1))
    down = a["ffn_w3"].reshape(groups, GROUP, HIDDEN, C).transpose(0, 2, 1, 3).reshape(groups, HIDDEN, GROUP * C)
    ffn = np.concatenate([up, down], axis=2)

    nc = bacc.Bacc("TRN2", target_bir_lowering=False, num_devices=1)
    arrays, args = {}, []
    for name, v in (("img", img), ("tokw", tokw), ("small", small), ("ffn", ffn)):
        arrays[f"in_{name}"] = np.ascontiguousarray(v)
        args.append(nc.dram_tensor(f"in_{name}", v.shape, F32, kind="ExternalInput").ap())
    args.append(nc.dram_tensor("out_dram", _OUT, F32, kind="ExternalOutput").ap())
    vit_tower(nc, *args)
    r = run_bass_kernel_spmd(nc, [arrays], core_ids=[0])
    return r.results[0]["out_dram"]
```

```python
from contextlib import ExitStack

import concourse.bass as bass
from concourse import mybir

ALU = mybir.AluOpType
ACT = mybir.ActivationFunctionType
F32 = mybir.dt.float32
F32R = mybir.dt.float32r
U32 = mybir.dt.uint32
AX_X = mybir.AxisListType.X

IMAGES, SIDE = 64, 96
PH, PW, STRIDE = 64, 25, 12
SEQ = (SIDE - PW) // STRIDE + 1
C = 64
COLS = STRIDE * (SEQ - 1) + PW
HCOLS = (COLS + 1) // 2
HSTEP = STRIDE // 2
TAPS = (PW + 1) // 2

TILE_IMAGES = 16
TOK = TILE_IMAGES * SEQ
TILES = IMAGES // TILE_IMAGES
CHUNK = 2
CHUNKS = TILES // CHUNK
CTOK = CHUNK * TOK
ALL = TILES * TOK
MASKED = -1.0e30

EXPERTS, HIDDEN, TOP = 16, 128, 2
GROUP = 4
EPS = 1e-5
FFN_COLS = 2 * GROUP * HIDDEN + GROUP * C
WARM = 8
WARM1, WARM2 = 3, 1
KEEP, KEEP1, KEEP2 = 9, 1, 1
ROUND = (6, 8, 10, 10)
RING = 8
PRING = 4
DOWN_AFTER = (6, 8, 9, 11, 12, 14, 15, 15)
SUMMED = EXPERTS // 2 - 2

SMALL, SMALL_COLS = {}, 0
for _name, _rows, _n in (("tokb", 128, 1), ("ln1_b", C, 1), ("ln1_g", C, 1), ("scale", TOK, 1), ("qkv", C + 1, 3 * C),
                         ("proj", C + 1, C), ("ln2_g", C + 1, C), ("ln2_b", TOK, C), ("rel", TOK, SEQ),
                         ("gate_w", 128, EXPERTS), ("gate_b", 1, EXPERTS)):
    SMALL[_name] = (_rows, SMALL_COLS, _n)
    SMALL_COLS += _n


def vit_tower(nc, img_in, tokw_in, small_in, ffn_in, out):
    with ExitStack() as ctx:
        def sb(name, shape, dt=F32):
            return ctx.enter_context(nc.sbuf_tensor(name, shape, dt))

        def bank(name):
            return ctx.enter_context(nc.psum_tensor(name, [128, 512], F32))

        def sem(name):
            return ctx.enter_context(nc.semaphore(name))

        ps_a = [bank(f"ps_a{c}") for c in range(CHUNKS)]
        ps_b = [bank(f"ps_b{c}") for c in range(CHUNKS)]
        ps_c = [bank(f"ps_c{c}") for c in range(CHUNKS)]
        ps_p = bank("ps_p")
        ps_d = bank("ps_d")
        ps_o = [ps_p, ps_d]

        img = sb("img", [128, IMAGES, HCOLS])
        tokw = sb("tokw", [128, TAPS, C])
        small = sb("small", [128, SMALL_COLS])
        warm = sb("warm", [128, 512], mybir.dt.bfloat16)
        ident = sb("ident", [128, 128])
        fold2 = sb("fold2", [128, C])
        half_neg = sb("half_neg", [128, TILES])
        lnL = sb("lnL", [C + 1, C + 1])
        wT = sb("wT", [C, 3, C + 1])
        G = sb("G", [C + 1, C + 1])
        projm = sb("projm", [C + 1, 1])
        projX = sb("projX", [C + 1, 2 * C])
        VW = sb("VW", [C + 1, 2 * C])
        relmask = sb("relmask", [TOK, TOK])
        ones_row = sb("ones_row", [1, TOK])
        iota16 = sb("iota16", [TOK, EXPERTS])
        sel = sb("sel", [2 * EXPERTS, EXPERTS])
        selr = sb("selr", [2 * EXPERTS, EXPERTS, C], F32R)

        gT = sb("gT", [128, CHUNKS, TOK])
        h0b = sb("h0b", [TOK, TILES, C])
        y = sb("y", [TOK, TILES, C])
        yT = sb("yT", [C + 1, ALL])
        Z = sb("Z", [C + 1, ALL])
        V = sb("V", [TOK + 1, TILES, 2 * C])
        P = sb("P", [TOK, TILES, TOK + 1])
        PT = sb("PT", [TOK + 1, TILES, TOK])
        h1 = sb("h1", [TOK, TILES, C])
        x3 = sb("x3", [TOK, TILES, 2, C])
        xs = sb("xs", [128, ALL], F32R)
        stats = sb("stats", [TOK, 3, TILES, 6])
        mv = sb("mv", [TOK, 3, TILES, 2])
        ve = sb("ve", [TOK, 3, TILES])
        rstd = sb("rstd", [TOK, 3, TILES])
        nmax = sb("nmax", [TOK, TILES])
        eps_sum2 = sb("eps_sum2", [TOK, TILES])

        top8 = sb("top8", [TOK, TILES, 8])
        idx8 = sb("idx8", [TOK, TILES, 8], U32)
        gap = sb("gap", [TOK, TILES])
        tnh = sb("tnh", [TOK, TILES])
        wtop = sb("wtop", [TOK, TILES, TOP])
        hot = sb("hot", [TOK, TILES, TOP, EXPERTS])
        disp = sb("disp", [TOK, TILES, EXPERTS])
        dsp = sb("dsp", [TOK, TILES, 2, EXPERTS], F32R)
        dT = sb("dT", [2 * EXPERTS, ALL], F32R)
        D = sb("D", [128, 2, ALL])

        ffn = sb("ffn", [128, EXPERTS // GROUP, FFN_COLS])
        whi = sb("whi", [128, 2, EXPERTS, HIDDEN], F32R)
        wlo = sb("wlo", [128, 2, EXPERTS, HIDDEN], F32R)
        sil = sb("sil", [HIDDEN, RING, ALL])
        hid = sb("hid", [HIDDEN, RING, ALL])
        prod = sb("prod", [128, PRING, ALL])
        acc = sb("acc", [128, 2, ALL])
        res = sb("res", [TOK, TILES, C])

        def part(name):
            rows, c0, n = SMALL[name]
            return small[0:rows, c0:c0 + n]

        tokb, lnb, g1col, qkvR, projR, g2row, b2row, scale_c, rel_rows, gate_w2, gate_row = (
            part(n) for n in ("tokb", "ln1_b", "ln1_g", "qkv", "proj", "ln2_g", "ln2_b", "scale", "rel",
                              "gate_w", "gate_b"))

        def raw12(e):
            return ffn[:, e // GROUP, 0:2 * GROUP * HIDDEN].rearrange(
                "p (i e h) -> p i e h", i=2, e=GROUP)[:, :, e % GROUP, :]

        def w3_of(e):
            c0 = 2 * GROUP * HIDDEN + (e % GROUP) * C
            return ffn[:, e // GROUP, c0:c0 + C]

        s_tokw, s_small, s_out = sem("s_tokw"), sem("s_small"), sem("s_out")
        s_img = [sem(f"s_img{t}") for t in range(TILES)]
        s_ffn = [sem(f"s_ffn{g}") for g in range(EXPERTS // GROUP)]
        warm_ready = sem("warm_ready")
        pool_const = sem("pool_const")
        ident_ready = sem("ident_ready")
        mask_ready = sem("mask_ready")
        sel_ready = sem("sel_ready")
        half_ready = sem("half_ready")
        ones_ready = sem("ones_ready")
        fold_ready = sem("fold_ready")
        lnL_ready = sem("lnL_ready")
        projX_ready = sem("projX_ready")
        wT_psum, wT_ready = sem("wT_psum"), sem("wT_ready")
        GV_psum, GV_ready = sem("GV_psum"), sem("GV_ready")
        conv_done, gelu_done, h0_done = sem("conv_done"), sem("gelu_done"), sem("h0_done")
        ve_ready, rstd_ready = sem("ve_ready"), sem("rstd_ready")
        h0b_ready = sem("h0b_ready")
        y_ready, yT_psum, yT_ready = sem("y_ready"), sem("yT_psum"), sem("yT_ready")
        Z_psum, Z_ready, V_psum, V_ready = sem("Z_psum"), sem("Z_ready"), sem("V_psum"), sem("V_ready")
        score_done, max_ready, exp_done = sem("score_done"), sem("max_ready"), sem("exp_done")
        PT_psum, PT_ready = sem("PT_psum"), sem("PT_ready")
        attn_done, h1_ready, x3_ready = sem("attn_done"), sem("h1_ready"), sem("x3_ready")
        xT_psum, xs_round, xs_ready = sem("xT_psum"), sem("xs_round"), sem("xs_ready")
        logit_done, gap_ready, tanh_done = sem("logit_done"), sem("gap_ready"), sem("tanh_done")
        disp_ready, dT_psum, dT_ready = sem("disp_ready"), sem("dT_psum"), sem("dT_ready")
        D_psum, D_ready = sem("D_psum"), sem("D_ready")
        whi_ready, wlo_ready = sem("whi_ready"), sem("wlo_ready")
        up1_done, up2_done, silu_done, hid_ready = sem("up1_done"), sem("up2_done"), sem("silu_done"), sem("hid_ready")
        down_done, prod_ready, acc_done = sem("down_done"), sem("prod_ready"), sem("acc_done")
        res_psum, res_ready = sem("res_psum"), sem("res_ready")
        dve_step = sem("dve_step")
        pool_step = sem("pool_step")

        out_dst = out.rearrange("(t i) n d -> (i n) t d", t=TILES)

        block = ctx.enter_context(nc.Block())

        @block.sync
        def _(sp):
            sp.dma_start(tokw[:], tokw_in).then_inc(s_tokw, 16)
            for t in range(TILES):
                b = slice(t * TILE_IMAGES, (t + 1) * TILE_IMAGES)
                sp.dma_start(img[:, b, :], img_in[t]).then_inc(s_img[t], 16)
            for g in range(EXPERTS // GROUP):
                sp.dma_start(ffn[:, g, :], ffn_in[g]).then_inc(s_ffn[g], 16)
            sp.wait_ge(res_ready, 1)
            sp.dma_start(out_dst, res[:]).then_inc(s_out, 16)
            sp.wait_ge(s_out, 16)

        @block.gpsimd
        def _(pool):
            n_step = [0]

            def link(ins):
                n_step[0] += 1
                ins.then_inc(pool_step, 1)
                pool.wait_ge(pool_step, n_step[0])

            nc.gpsimd.memset(half_neg[:], -0.5).then_inc(half_ready, 1)
            link(nc.gpsimd.memset(ident[:], 0.0))
            nc.gpsimd.affine_select(out=ident[:], in_=ident[:], compare_op=ALU.not_equal, fill=1.0, base=0,
                                    pattern=[[-1, 128]], channel_multiplier=1).then_inc(ident_ready, 1)
            nc.gpsimd.memset(ones_row[:], 1.0).then_inc(ones_ready, 1)
            pool.wait_ge(s_small, 16)
            rel_b = rel_rows.rearrange("p (a j) -> p a j", a=1).to_broadcast([TOK, TILE_IMAGES, SEQ])
            mask3 = relmask[:].rearrange("p (b j) -> p b j", j=SEQ)
            link(nc.gpsimd.affine_select(out=mask3, in_=rel_b, compare_op=ALU.is_ge, fill=MASKED, base=0,
                                         pattern=[[-SEQ, TILE_IMAGES], [0, SEQ]], channel_multiplier=1))
            nc.gpsimd.affine_select(out=mask3, in_=mask3, compare_op=ALU.is_ge, fill=MASKED, base=SEQ - 1,
                                    pattern=[[SEQ, TILE_IMAGES], [0, SEQ]], channel_multiplier=-1
                                    ).then_inc(mask_ready, 1)
            nc.gpsimd.iota(iota16[:], pattern=[[1, EXPERTS]], base=0, channel_multiplier=0,
                           allow_small_or_imprecise_dtypes=True).then_inc(pool_const, 1)

            def low_part(e):
                pool.wait_ge(whi_ready, e + 1)
                nc.gpsimd.tensor_tensor(wlo[:, :, e, :], raw12(e), whi[:, :, e, :].bitcast(F32),
                                        ALU.subtract).then_inc(wlo_ready, 1)

            def power(k, c, n):
                pool.wait_ge(ve_ready, n)
                t = slice(c * CHUNK, (c + 1) * CHUNK)
                nc.gpsimd.tensor_tensor(rstd[:, k, t], ve[:, k, t], half_neg[0:TOK, t],
                                        ALU.pow).then_inc(rstd_ready, 1)

            def add_pair(p):
                pool.wait_ge(prod_ready, p + 1)
                if p >= 2:
                    pool.wait_ge(acc_done, p - 1)
                before = prod[:, 0, :] if p == 1 else acc[:, (p - 1) % 2, :]
                nc.gpsimd.tensor_tensor(acc[:, p % 2, :], before, prod[:, p % PRING, :], ALU.add).then_inc(acc_done, 1)

            for n, (k, c) in enumerate(LN_ORDER):
                power(k, c, n + 1)
                for e in range(LOW_AFTER[n], LOW_AFTER[n + 1]):
                    low_part(e)
            for p in range(1, SUMMED):
                add_pair(p)

        @block.scalar
        def _(act):
            act.dma_start(small[:], small_in).then_inc(s_small, 16)
            nc.scalar.preload_act_table(ACT.Gelu)
            act.wait_ge(s_small, 16)

            def round_weights(experts):
                for e in experts:
                    if e % GROUP == 0:
                        act.wait_ge(s_ffn[e // GROUP], 16)
                    nc.scalar.copy(whi[:, :, e, :], raw12(e)).then_inc(whi_ready, 1)

            for c in range(CHUNKS):
                act.wait_ge(conv_done, c + 1)
                nc.scalar.activation(gT[:, c, :], ps_a[c][:, 0:TOK], ACT.Gelu, bias=tokb
                                     ).then_inc(gelu_done, 1)
                if c == 0:
                    round_weights(range(0, ROUND[0]))
            nc.scalar.preload_act_table(ACT.Exp)
            round_weights(range(ROUND[0], ROUND[1]))
            for c in range(CHUNKS):
                t0 = c * CHUNK
                act.wait_ge(max_ready, c + 1)
                for t in range(CHUNK):
                    nc.scalar.activation(P[:, t0 + t, 0:TOK], ps_c[c][0:TOK, t * TOK:(t + 1) * TOK], ACT.Exp,
                                         bias=nmax[:, t0 + t:t0 + t + 1],
                                         accum_out=P[:, t0 + t, TOK:TOK + 1]).then_inc(exp_done, 1)
                act.wait_ge(V_psum, c + 1)
                nc.scalar.copy(V[0:TOK, t0:t0 + CHUNK, :], ps_b[c][0:TOK, 0:CHUNK * 2 * C].rearrange(
                    "p (t n) -> p t n", t=CHUNK)).then_inc(V_ready, 1)
                round_weights(range(ROUND[1 + c], ROUND[2 + c]))
            nc.scalar.preload_act_table(ACT.Silu)
            round_weights(range(ROUND[3], EXPERTS))
            for c in range(CHUNKS):
                act.wait_ge(xT_psum, c + 1)
                nc.scalar.copy(xs[:, c * CTOK:(c + 1) * CTOK], ps_b[c][:, 0:CTOK]).then_inc(xs_round, 1)

            def spread(p):
                act.wait_ge(D_psum, p + 1)
                if p >= 2:
                    act.wait_ge(prod_ready, p - 1)
                nc.scalar.copy(D[:, p % 2, :], ps_o[p % 2][:, 0:ALL]).then_inc(D_ready, 1)

            for e in range(EXPERTS):
                act.wait_ge(up1_done, e + 1)
                if e >= RING:
                    act.wait_ge(hid_ready, e - RING + 1)
                nc.scalar.activation(sil[:, e % RING, :], ps_c[e % 2][:, 0:ALL], ACT.Silu).then_inc(silu_done, 1)
                if e == 1:
                    act.wait_ge(gap_ready, 1)
                    nc.scalar.activation(tnh[:], gap[:], ACT.Tanh, scale=0.5).then_inc(tanh_done, 1)
                for p in pairs_after(e - 1):
                    spread(p)
            for p in pairs_after(EXPERTS - 1):
                spread(p)

        @block.vector
        def _(dve):
            n_step = [0]

            def step(*instructions):
                for ins in instructions:
                    n_step[0] += 1
                    ins.then_inc(dve_step, 1)

            def caught_up():
                dve.wait_ge(dve_step, n_step[0])

            def link(*instructions):
                step(*instructions)
                caught_up()

            nc.vector.memset(warm[:], 0.0).then_inc(warm_ready, 1)
            nc.vector.memset(lnL[C:C + 1, 0:C], 0.0).then_inc(lnL_ready, 1)
            nc.vector.memset(lnL[C:C + 1, C:C + 1], 1.0).then_inc(lnL_ready, 1)
            nc.vector.memset(yT[C:C + 1, :], 1.0).then_inc(lnL_ready, 1)
            dve.wait_ge(ident_ready, 1)
            nc.vector.tensor_tensor(fold2[:], ident[:, 0:C], ident[:, C:128], ALU.add).then_inc(fold_ready, 1)
            dve.wait_ge(s_small, 16)
            nc.vector.tensor_copy(lnL[0:C, C:C + 1], lnb).then_inc(lnL_ready, 1)
            nc.vector.tensor_scalar(lnL[0:C, 0:C], ident[0:C, 0:C], g1col, None, ALU.mult
                                    ).then_inc(lnL_ready, 1)
            link(nc.vector.tensor_reduce(projm[:], projR, AX_X, ALU.add))
            link(nc.vector.tensor_scalar(projm[:], projm[:], 1.0 / C, None, ALU.mult))
            link(nc.vector.tensor_scalar(projX[:, 0:C], projR, projm[:, 0:1], None, ALU.subtract))
            nc.vector.tensor_tensor(projX[:, C:2 * C], projX[:, 0:C], g2row, ALU.mult).then_inc(projX_ready, 1)
            dve.wait_ge(wT_psum, 1)
            nc.vector.tensor_copy(wT[:], ps_p[0:C, 0:3 * (C + 1)].rearrange("p (i n) -> p i n", i=3)
                                  ).then_inc(wT_ready, 1)
            dve.wait_ge(GV_psum, 1)
            nc.vector.tensor_copy(G[:], ps_d[0:C + 1, 0:C + 1]).then_inc(GV_ready, 1)
            nc.vector.tensor_scalar(VW[:], ps_d[0:C + 1, 128:128 + 2 * C], scale_c[0:C + 1, :], None, ALU.mult
                                    ).then_inc(GV_ready, 1)
            nc.vector.tensor_copy(V[TOK:TOK + 1, :, :], projX[C:C + 1, :].rearrange("p (a n) -> p a n", a=1)
                                  .to_broadcast([1, TILES, 2 * C])).then_inc(GV_ready, 1)
            link(nc.vector.tensor_tensor(sel[:], ident[0:2 * EXPERTS, 0:EXPERTS],
                                         ident[0:2 * EXPERTS, EXPERTS:2 * EXPERTS], ALU.add))
            nc.vector.tensor_copy(selr[:], sel[:].rearrange("p (e a) -> p e a", a=1).to_broadcast(
                [2 * EXPERTS, EXPERTS, C])).then_inc(fold_ready, 1)

            def bn(sources, k, c):
                t0 = c * CHUNK
                link(*[nc.vector.bn_stats(stats[:, k, t0 + t, :], sources[t]) for t in range(CHUNK)])
                link(*[nc.vector.bn_aggr(mv[:, k, t0 + t, :], stats[:, k, t0 + t, :]) for t in range(CHUNK)])

            def normal_stats(k, c, sources, mul, add):
                t0 = c * CHUNK
                bn(sources, k, c)
                nc.vector.tensor_scalar(ve[:, k, t0:t0 + CHUNK], mv[:, k, t0:t0 + CHUNK, 1], mul, add,
                                        ALU.mult, ALU.add).then_inc(ve_ready, 1)

            def h0_of(c):
                return [ps_a[c][0:TOK, 128 + t * C:128 + (t + 1) * C] for t in range(CHUNK)]

            def stats_in(c):
                dve.wait_ge(h0_done, c + 1)
                h0 = h0_of(c)
                normal_stats(0, c, h0, 1.0 + EPS, EPS * EPS)
                for t in range(CHUNK):
                    nc.vector.tensor_tensor(h0b[:, c * CHUNK + t, :], h0[t], b2row, ALU.add).then_inc(h0b_ready, 1)

            def norm_in(c):
                dve.wait_ge(rstd_ready, LN_ORDER.index((0, c)) + 1)
                for t in range(CHUNK):
                    g = c * CHUNK + t
                    nc.vector.tensor_scalar(y[:, g, :], h0_of(c)[t], mv[:, 0, g, 0:1], rstd[:, 0, g:g + 1],
                                            ALU.subtract, ALU.mult).then_inc(y_ready, 1)

            def copy_yT(c):
                dve.wait_ge(yT_psum, c + 1)
                nc.vector.tensor_copy(yT[0:C, c * CTOK:(c + 1) * CTOK], ps_a[c][0:C, 256:256 + CTOK]
                                      ).then_inc(yT_ready, 1)

            def copy_Z(c):
                dve.wait_ge(Z_psum, c + 1)
                nc.vector.tensor_copy(Z[:, c * CTOK:(c + 1) * CTOK], ps_a[c][0:C + 1, 0:CTOK]).then_inc(Z_ready, 1)

            def row_max(c):
                t0 = c * CHUNK
                dve.wait_ge(score_done, c + 1)
                nc.vector.tensor_reduce(nmax[:, t0:t0 + CHUNK],
                                        ps_c[c][0:TOK, 0:CTOK].rearrange("p (t m) -> p t m", t=CHUNK),
                                        AX_X, ALU.max, negate=True).then_inc(max_ready, 1)

            def square_sums(c):
                t = slice(c * CHUNK, (c + 1) * CHUNK)
                dve.wait_ge(exp_done, CHUNK * (c + 1))
                step(nc.vector.scalar_tensor_tensor(eps_sum2[:, t], P[:, t, TOK], EPS, P[:, t, TOK],
                                                    ALU.mult, ALU.mult))

            def copy_PT(c):
                t0 = c * CHUNK
                dve.wait_ge(PT_psum, c + 1)
                nc.vector.tensor_copy(PT[:, t0:t0 + CHUNK, :], ps_a[c][0:TOK + 1, 0:CTOK].rearrange(
                    "p (t m) -> p t m", t=CHUNK)).then_inc(PT_ready, 1)

            def attn_of(c):
                return [ps_o[c][0:TOK, t * 2 * C:t * 2 * C + 2 * C] for t in range(CHUNK)]

            def stats_out(c):
                dve.wait_ge(attn_done, c + 1)
                t0 = c * CHUNK
                bn([v[:, 0:C] for v in attn_of(c)], 1, c)
                nc.vector.tensor_tensor(ve[:, 1, t0:t0 + CHUNK], mv[:, 1, t0:t0 + CHUNK, 1],
                                        eps_sum2[:, t0:t0 + CHUNK], ALU.add).then_inc(ve_ready, 1)

            def residual(c):
                t0 = c * CHUNK
                dve.wait_ge(h0b_ready, CHUNK * (c + 1))
                dve.wait_ge(rstd_ready, LN_ORDER.index((1, c)) + 1)
                step(*[nc.vector.scalar_tensor_tensor(h1[:, t0 + t, :], attn_of(c)[t][:, C:2 * C],
                                                      rstd[:, 1, t0 + t:t0 + t + 1], h0b[:, t0 + t, :],
                                                      ALU.mult, ALU.add) for t in range(CHUNK)])

            def stats_x(c):
                t0 = c * CHUNK
                caught_up()
                normal_stats(2, c, [h1[:, t0 + t, :] for t in range(CHUNK)], 1.0, EPS)

            def norm_x(c):
                dve.wait_ge(rstd_ready, LN_ORDER.index((2, c)) + 1)
                for t in range(CHUNK):
                    g = c * CHUNK + t
                    nc.vector.tensor_scalar(x3[:, g, :, :], h1[:, g:g + 1, :].to_broadcast([TOK, 2, C]),
                                            mv[:, 2, g, 0:1], rstd[:, 2, g:g + 1], ALU.subtract, ALU.mult
                                            ).then_inc(x3_ready, 1)

            def split_x(c):
                cols = slice(c * CTOK, (c + 1) * CTOK)
                dve.wait_ge(xs_round, c + 1)
                nc.vector.tensor_tensor(xs[C:128, cols], ps_b[c][C:128, 0:CTOK], xs[C:128, cols].bitcast(F32),
                                        ALU.subtract).then_inc(xs_ready, 1)

            stats_in(0)
            norm_in(0)
            copy_yT(0)
            stats_in(1)
            copy_Z(0)
            norm_in(1)
            row_max(0)
            copy_yT(1)
            square_sums(0)
            copy_Z(1)
            copy_PT(0)
            row_max(1)
            stats_out(0)
            square_sums(1)
            copy_PT(1)
            residual(0)
            stats_out(1)
            stats_x(0)
            residual(1)
            stats_x(1)
            norm_x(0)
            norm_x(1)
            split_x(0)
            split_x(1)

            def hidden(e):
                dve.wait_ge(silu_done, e + 1)
                dve.wait_ge(up2_done, e + 1)
                if e >= RING:
                    dve.wait_ge(down_done, (e - RING) // 2 + 1)
                nc.vector.tensor_tensor(hid[:, e % RING, :], ps_a[e % 2][:, 0:ALL], sil[:, e % RING, :], ALU.mult
                                        ).then_inc(hid_ready, 1)

            def weigh(p):
                dve.wait_ge(down_done, p + 1)
                dve.wait_ge(D_ready, p + 1)
                if p >= PRING:
                    dve.wait_ge(acc_done, max(p - PRING, 1))
                nc.vector.tensor_tensor(prod[:, p % PRING, :], ps_b[p % 2][:, 0:ALL], D[:, p % 2, :], ALU.mult
                                        ).then_inc(prod_ready, 1)

            hidden(0)
            dve.wait_ge(logit_done, 1)
            lg = ps_p[0:TOK, 0:TILES * EXPERTS].rearrange("p (t e) -> p t e", t=TILES)
            link(*[nc.vector.max(top8[:, t, :], lg[:, t, :]) for t in range(TILES)])
            nc.vector.tensor_tensor(gap[:], top8[:, :, 0], top8[:, :, 1], ALU.subtract).then_inc(gap_ready, 1)
            step(*[nc.vector.max_index(idx8[:, t, :], top8[:, t, :], lg[:, t, :]) for t in range(TILES)])
            hidden(1)
            caught_up()
            dve.wait_ge(pool_const, 1)
            step(*[nc.vector.tensor_tensor(
                hot[:, :, k, :],
                iota16[:].rearrange("p (a e) -> p a e", a=1).to_broadcast([TOK, TILES, EXPERTS]),
                idx8[:, :, k:k + 1].to_broadcast([TOK, TILES, EXPERTS]), ALU.is_equal) for k in range(TOP)])
            dve.wait_ge(tanh_done, 1)
            step(nc.vector.tensor_scalar(wtop[:, :, 0], tnh[:], 0.5, 0.5, ALU.mult, ALU.add),
                 nc.vector.tensor_scalar(wtop[:, :, 1], tnh[:], -0.5, 0.5, ALU.mult, ALU.add))
            hidden(2)
            caught_up()
            step(*[nc.vector.tensor_tensor(hot[:, :, k, :], hot[:, :, k, :],
                                           wtop[:, :, k:k + 1].to_broadcast([TOK, TILES, EXPERTS]), ALU.mult)
                   for k in range(TOP)])
            hidden(3)
            caught_up()
            link(nc.vector.tensor_tensor(disp[:], hot[:, :, 0, :], hot[:, :, 1, :], ALU.add))
            link(nc.vector.tensor_copy(dsp[:, :, 0, :], disp[:]))
            nc.vector.tensor_tensor(dsp[:, :, 1, :], disp[:], dsp[:, :, 0, :].bitcast(F32), ALU.subtract
                                    ).then_inc(disp_ready, 1)
            hidden(4)
            dve.wait_ge(dT_psum, 1)
            nc.vector.tensor_copy(dT[:], ps_p[0:2 * EXPERTS, 0:ALL]).then_inc(dT_ready, 1)
            for e in range(5, EXPERTS):
                hidden(e)
                for p in pairs_after(e):
                    weigh(p)
            dve.wait_ge(res_psum, 1)
            nc.vector.tensor_tensor(res[:], ps_c[0][0:TOK, 0:TILES * C].rearrange("p (t d) -> p t d", t=TILES),
                                    h1[:], ALU.add).then_inc(res_ready, 1)

        @block.tensor
        def _(pe):
            mm = nc.tensor.matmul

            def keep_clock(n, free_bank):
                for _ in range(n):
                    mm(free_bank[:], warm[:, 0:128], warm[:], start=True, stop=True)

            pe.wait_ge(warm_ready, 1)
            keep_clock(WARM, ps_b[1])
            pe.wait_ge(lnL_ready, 5)
            for i in range(3):
                last = mm(ps_p[0:C, i * (C + 1):(i + 1) * (C + 1)], qkvR[:, i * C:(i + 1) * C], lnL[:],
                          start=True, stop=True)
            last.then_inc(wT_psum, 1)
            keep_clock(WARM1, ps_b[1])
            pe.wait_ge(wT_ready, 1)
            pe.wait_ge(projX_ready, 1)
            mm(ps_d[0:C + 1, 0:C + 1], wT[:, 0, :], wT[:, 1, :], start=True, stop=True)
            mm(ps_d[0:C + 1, 128:128 + 2 * C], wT[:, 2, :], projX[0:C, :], start=True, stop=True
               ).then_inc(GV_psum, 1)
            def conv(c, taps):
                if taps[0] == 0:
                    for t in range(CHUNK):
                        pe.wait_ge(s_img[c * CHUNK + t], 16)
                for j in taps:
                    k = 128 if j < TAPS - 1 else C
                    for t in range(CHUNK):
                        b0 = (c * CHUNK + t) * TILE_IMAGES
                        patch = img[0:k, b0:b0 + TILE_IMAGES, j:j + HSTEP * (SEQ - 1) + 1:HSTEP]
                        last = mm(ps_a[c][t * C:(t + 1) * C, 0:TOK].rearrange("p (b n) -> p b n", n=SEQ),
                                  tokw[0:k, j, :], patch, start=(j == 0), stop=(j == TAPS - 1))
                if taps[-1] == TAPS - 1:
                    last.then_inc(conv_done, 1)

            def to_tokens(c):
                pe.wait_ge(gelu_done, c + 1)
                nc.tensor.transpose(ps_a[c][0:TOK, 128:256], gT[:, c, :], ident[:]).then_inc(h0_done, 1)

            def y_to_T(c):
                pe.wait_ge(y_ready, CHUNK * (c + 1))
                for t in range(CHUNK):
                    last = nc.tensor.transpose(ps_a[c][0:C, 256 + t * TOK:256 + (t + 1) * TOK],
                                               y[:, c * CHUNK + t, :], ident[0:TOK, 0:TOK])
                last.then_inc(yT_psum, 1)

            def project(c):
                cols = slice(c * CTOK, (c + 1) * CTOK)
                pe.wait_ge(yT_ready, c + 1)
                mm(ps_a[c][0:C + 1, 0:CTOK], G[:], yT[:, cols], start=True, stop=True).then_inc(Z_psum, 1)

            def values(c):
                for t in range(CHUNK):
                    tok = slice(c * CTOK + t * TOK, c * CTOK + (t + 1) * TOK)
                    last = mm(ps_b[c][0:TOK, t * 2 * C:(t + 1) * 2 * C], yT[:, tok], VW[:], start=True, stop=True)
                last.then_inc(V_psum, 1)

            def scores(c):
                pe.wait_ge(Z_ready, c + 1)
                for t in range(CHUNK):
                    tok = slice(c * CTOK + t * TOK, c * CTOK + (t + 1) * TOK)
                    last = mm(ps_c[c][0:TOK, t * TOK:(t + 1) * TOK], Z[:, tok], yT[:, tok],
                              start=False, stop=(t == CHUNK - 1), skip_group_check=True)
                last.then_inc(score_done, 1)

            def P_to_T(c):
                pe.wait_ge(exp_done, CHUNK * (c + 1))
                for t in range(CHUNK):
                    last = nc.tensor.transpose(ps_a[c][0:TOK + 1, t * TOK:(t + 1) * TOK], P[:, c * CHUNK + t, :],
                                               ident[0:TOK, 0:TOK])
                last.then_inc(PT_psum, 1)

            def attend(c):
                pe.wait_ge(PT_ready, c + 1)
                pe.wait_ge(V_ready, c + 1)
                for t in range(CHUNK):
                    last = mm(ps_o[c][0:TOK, t * 2 * C:(t + 1) * 2 * C], PT[:, c * CHUNK + t, :],
                              V[:, c * CHUNK + t, :], start=True, stop=True)
                last.then_inc(attn_done, 1)

            def x_to_T(c):
                pe.wait_ge(x3_ready, CHUNK * (c + 1))
                for t in range(CHUNK):
                    last = nc.tensor.transpose(ps_b[c][:, t * TOK:(t + 1) * TOK],
                                               x3[:, c * CHUNK + t, :, :].rearrange("p a d -> p (a d)"),
                                               ident[0:TOK, 0:TOK])
                last.then_inc(xT_psum, 1)

            keep_clock(WARM2, ps_b[1])
            pe.wait_ge(s_tokw, 16)
            conv(0, range(TAPS))
            conv(1, range(3))
            to_tokens(0)
            conv(1, range(3, TAPS))
            pe.wait_ge(GV_ready, 3)
            y_to_T(0)
            to_tokens(1)
            pe.wait_ge(mask_ready, 1)
            for c in range(CHUNKS):
                two = relmask[:].rearrange("p (a m) -> p a m", a=1).to_broadcast([TOK, CHUNK, TOK])
                mm(ps_c[c][0:TOK, 0:CTOK].rearrange("p (t m) -> p t m", t=CHUNK), ident[0:TOK, 0:TOK], two,
                   start=True, stop=False, skip_group_check=True)
            project(0)
            values(0)
            scores(0)
            y_to_T(1)
            project(1)
            P_to_T(0)
            scores(1)
            attend(0)
            values(1)
            P_to_T(1)
            attend(1)
            keep_clock(KEEP, ps_c[0])
            x_to_T(0)
            keep_clock(KEEP1, ps_c[0])
            x_to_T(1)
            keep_clock(KEEP2, ps_c[0])

            def logits():
                gate_b4 = gate_row.rearrange("p (a e) -> p a e", a=1).to_broadcast([1, TILES, EXPERTS])
                mm(ps_p[0:TOK, 0:TILES * EXPERTS].rearrange("p (t e) -> p t e", t=TILES), ones_row[:], gate_b4,
                   start=True, stop=False, skip_group_check=True)
                for t in range(TILES):
                    last = mm(ps_p[0:TOK, t * EXPERTS:(t + 1) * EXPERTS],
                              xs[:, t * TOK:(t + 1) * TOK].bitcast(F32), gate_w2,
                              start=False, stop=(t == TILES - 1), skip_group_check=True)
                last.then_inc(logit_done, 1)

            def up(i, e, dst, done):
                pe.wait_ge(whi_ready, e + 1)
                pe.wait_ge(wlo_ready, e + 1)
                mm(dst[:, 0:ALL], whi[:, i, e, :], xs[:], start=True, stop=False)
                mm(dst[:, 0:ALL], wlo[:, i, e, :], xs[:], start=False, stop=True).then_inc(done, 1)

            def up1(e):
                if e >= 2:
                    pe.wait_ge(silu_done, e - 1)
                up(0, e, ps_c[e % 2], up1_done)

            def up2(e):
                if e >= 2:
                    pe.wait_ge(hid_ready, e - 1)
                up(1, e, ps_a[e % 2], up2_done)

            def spread_dispatch(p):
                if p >= 2:
                    pe.wait_ge(D_ready, p - 1)
                mm(ps_o[p % 2][:, 0:ALL], selr[:, 2 * p:2 * p + 2, :].rearrange("p a n -> p (a n)"), dT[:],
                   start=True, stop=True).then_inc(D_psum, 1)

            def down(p):
                pe.wait_ge(s_ffn[2 * p // GROUP], 16)
                pe.wait_ge(hid_ready, 2 * p + 2)
                if p >= 2:
                    pe.wait_ge(prod_ready, p - 1)
                for h in range(2):
                    e = 2 * p + h
                    last = mm(ps_b[p % 2][h * C:(h + 1) * C, 0:ALL], w3_of(e), hid[:, e % RING, :],
                              start=True, stop=True)
                last.then_inc(down_done, 1)

            def dispatch_to_T():
                pe.wait_ge(disp_ready, 1)
                for t in range(TILES):
                    last = nc.tensor.transpose(ps_p[0:2 * EXPERTS, t * TOK:(t + 1) * TOK],
                                               dsp[:, t, :, :].rearrange("p s e -> p (s e)").bitcast(F32),
                                               ident[0:TOK, 0:TOK])
                last.then_inc(dT_psum, 1)

            pe.wait_ge(xs_ready, CHUNKS)
            pe.wait_ge(ones_ready, 1)
            up1(0)
            up1(1)
            for e in range(EXPERTS):
                up2(e)
                if e == 0:
                    logits()
                if e + 2 < EXPERTS:
                    up1(e + 2)
                if e == 4:
                    dispatch_to_T()
                if e == DOWN_AFTER[0]:
                    pe.wait_ge(dT_ready, 1)
                    pe.wait_ge(fold_ready, 2)
                pairs = pairs_after(e)
                for p in pairs:
                    spread_dispatch(p)
                for p in pairs:
                    down(p)
            folds = ((prod_ready, SUMMED + 1, prod[:, SUMMED % PRING, :]),
                     (acc_done, SUMMED - 1, acc[:, (SUMMED - 1) % 2, :]),
                     (prod_ready, SUMMED + 2, prod[:, (SUMMED + 1) % PRING, :]))
            for i, (done, n, part_sum) in enumerate(folds):
                pe.wait_ge(done, n)
                for t in range(TILES):
                    last = mm(ps_c[0][0:TOK, t * C:(t + 1) * C], part_sum[:, t * TOK:(t + 1) * TOK], fold2[:],
                              start=(i == 0 and t == 0), stop=(i == len(folds) - 1 and t == TILES - 1),
                              skip_group_check=True)
            last.then_inc(res_psum, 1)


def pairs_after(e):
    return [p for p, at in enumerate(DOWN_AFTER) if at == e]


LN_ORDER = [(0, 0), (0, 1), (1, 0), (1, 1), (2, 0), (2, 1)]
LOW_AFTER = [0, 3, 9, 9, 9, 10, EXPERTS]


_OUT = (IMAGES, SEQ, C)


def kernel(**inputs):
    import numpy as np
    from concourse import bacc
    from concourse.bass_utils import run_bass_kernel_spmd

    a = {k.replace("L0_", ""): np.asarray(v) for k, v in inputs.items()}

    def by_parity(v):
        odd = np.concatenate([v[..., 1::2], np.zeros_like(v[..., :1])], axis=-1)
        return v[..., 0::2], odd

    rows = a["x"][:, 0, 0:PH, 0:COLS].reshape(TILES, TILE_IMAGES, PH, COLS).transpose(0, 2, 1, 3)
    img = np.concatenate(by_parity(rows), axis=1)
    taps = a["tok_weight"].reshape(PH, PW, C).transpose(0, 2, 1)
    tokw = np.concatenate(by_parity(taps), axis=0).transpose(0, 2, 1)

    table = a["attn_bias_table"]
    rel = np.stack([table[SEQ - 1 - i:2 * SEQ - 1 - i] for i in range(SEQ)])
    pieces = {
        "tokb": np.tile(a["tok_bias"], 2)[:, None],
        "ln1_b": a["attn_ln1_b"][:, None],
        "ln1_g": a["attn_ln1_g"][:, None],
        "scale": np.broadcast_to(a["attn_scale"], (TOK, 1)),
        "qkv": np.concatenate([a["attn_qkv_w"], a["attn_qkv_b"][None]]),
        "proj": np.concatenate([a["attn_proj_w"], a["attn_proj_b"][None]]),
        "ln2_g": np.broadcast_to(a["attn_ln2_g"], (C + 1, C)),
        "ln2_b": np.broadcast_to(a["attn_ln2_b"], (TOK, C)),
        "rel": np.tile(rel, (TILE_IMAGES, 1)),
        "gate_w": np.tile(a["ffn_gate_w"], (2, 1)),
        "gate_b": a["ffn_gate_b"][None],
    }
    small = np.zeros((128, SMALL_COLS), np.float32)
    for name, (n, c0, cols) in SMALL.items():
        small[0:n, c0:c0 + cols] = pieces[name]

    groups = EXPERTS // GROUP
    up = np.stack([a["ffn_w1"], a["ffn_w2"]]).reshape(2, groups, GROUP, C, HIDDEN).transpose(1, 3, 0, 2, 4)
    up = np.tile(up.reshape(groups, C, 2 * GROUP * HIDDEN), (1, 2, 1))
    down = a["ffn_w3"].reshape(groups, GROUP, HIDDEN, C).transpose(0, 2, 1, 3).reshape(groups, HIDDEN, GROUP * C)
    ffn = np.concatenate([up, down], axis=2)

    nc = bacc.Bacc("TRN2", target_bir_lowering=False, num_devices=1)
    arrays, args = {}, []
    for name, v in (("img", img), ("tokw", tokw), ("small", small), ("ffn", ffn)):
        arrays[f"in_{name}"] = np.ascontiguousarray(v)
        args.append(nc.dram_tensor(f"in_{name}", v.shape, F32, kind="ExternalInput").ap())
    args.append(nc.dram_tensor("out_dram", _OUT, F32, kind="ExternalOutput").ap())
    vit_tower(nc, *args)
    r = run_bass_kernel_spmd(nc, [arrays], core_ids=[0])
    return r.results[0]["out_dram"]
```

```python
from contextlib import ExitStack

import concourse.bass as bass
from concourse import mybir

ALU = mybir.AluOpType
ACT = mybir.ActivationFunctionType
F32 = mybir.dt.float32
F32R = mybir.dt.float32r
U32 = mybir.dt.uint32
AX_X = mybir.AxisListType.X

IMAGES, SIDE = 64, 96
PH, PW, STRIDE = 64, 25, 12
SEQ = (SIDE - PW) // STRIDE + 1
C = 64
COLS = STRIDE * (SEQ - 1) + PW
HCOLS = (COLS + 1) // 2
HSTEP = STRIDE // 2
TAPS = (PW + 1) // 2

TILE_IMAGES = 16
TOK = TILE_IMAGES * SEQ
TILES = IMAGES // TILE_IMAGES
CHUNK = 2
CHUNKS = TILES // CHUNK
CTOK = CHUNK * TOK
ALL = TILES * TOK
MASKED = -1.0e30

EXPERTS, HIDDEN, TOP = 16, 128, 2
GROUP = 4
EPS = 1e-5
FFN_COLS = 2 * GROUP * HIDDEN + GROUP * C
FIRST_TAPS, FOLD_TAP = 5, 8
ZEROS_START, ZEROS_ATTENTION, ZEROS_EXPERTS = 9, (2, 3, 5, 2), (12, 2)
ROUND = (6, 8, 10, 10)
RING = 8
PRING = 4
DOWN_AFTER = (3, 5, 7, 9, 11, 13, 15, 15)
WEIGH_AFTER = (8, 9, 10, 11, 12, 13, 15, 15)
SUMMED = EXPERTS // 2 - 2

SMALL, SMALL_COLS = {}, 0
for _name, _rows, _n in (("tokb", 128, 1), ("ln1_b", C, 1), ("ln1_g", C, 1), ("scale", TOK, 1), ("qkv", C + 1, 3 * C),
                         ("proj", C + 1, C), ("ln2_g", C + 1, C), ("ln2_b", TOK, C), ("rel", TOK, SEQ),
                         ("gate_w", 128, EXPERTS), ("gate_b", 1, EXPERTS)):
    SMALL[_name] = (_rows, SMALL_COLS, _n)
    SMALL_COLS += _n


def vit_tower(nc, img_in, tokw_in, small_in, ffn_in, out):
    with ExitStack() as ctx:
        def sb(name, shape, dt=F32):
            return ctx.enter_context(nc.sbuf_tensor(name, shape, dt))

        def bank(name):
            return ctx.enter_context(nc.psum_tensor(name, [128, 512], F32))

        def sem(name):
            return ctx.enter_context(nc.semaphore(name))

        ps_a = [bank(f"ps_a{c}") for c in range(CHUNKS)]
        ps_b = [bank(f"ps_b{c}") for c in range(CHUNKS)]
        ps_c = [bank(f"ps_c{c}") for c in range(CHUNKS)]
        ps_p = bank("ps_p")
        ps_d = bank("ps_d")
        ps_y = ps_b + [ps_d, ps_p]
        ps_o = [ps_p, ps_d]

        img = sb("img", [128, IMAGES, HCOLS])
        tokw = sb("tokw", [128, TAPS, C])
        small = sb("small", [128, SMALL_COLS])
        warm = sb("warm", [128, 512], mybir.dt.bfloat16)
        ident = sb("ident", [128, 128])
        fold2 = sb("fold2", [128, C])
        half_neg = sb("half_neg", [128, TILES])
        lnL = sb("lnL", [C + 1, C + 1])
        wT = sb("wT", [C, 3, C + 1])
        G = sb("G", [C + 1, C + 1])
        projm = sb("projm", [C + 1, 1])
        projX = sb("projX", [C + 1, 2 * C])
        VW = sb("VW", [C + 1, 2 * C])
        relmask = sb("relmask", [TOK, TOK])
        ones_row = sb("ones_row", [1, TOK])
        iota16 = sb("iota16", [TOK, EXPERTS])

        gT = sb("gT", [128, CHUNKS, TOK])
        h0b = sb("h0b", [TOK, TILES, C])
        y = sb("y", [TOK, TILES, C])
        yT = sb("yT", [C + 1, ALL])
        Z = sb("Z", [C + 1, ALL])
        V = sb("V", [TOK + 1, TILES, 2 * C])
        P = sb("P", [TOK, TILES, TOK + 1])
        PT = sb("PT", [TOK + 1, TILES, TOK])
        h1 = sb("h1", [TOK, TILES, C])
        x3 = sb("x3", [TOK, TILES, 2, C])
        xs = sb("xs", [128, ALL], F32R)
        stats = sb("stats", [TOK, 3, TILES, 6])
        mv = sb("mv", [TOK, 3, TILES, 2])
        ve = sb("ve", [TOK, 3, TILES])
        rstd = sb("rstd", [TOK, 3, TILES])
        nmax = sb("nmax", [TOK, TILES])
        eps_sum2 = sb("eps_sum2", [TOK, TILES])

        top8 = sb("top8", [TOK, TILES, 8])
        idx8 = sb("idx8", [TOK, TILES, 8], U32)
        gap = sb("gap", [TOK, TILES])
        tnh = sb("tnh", [TOK, TILES])
        wtop = sb("wtop", [TOK, TILES, TOP])
        hot = sb("hot", [TOK, TILES, TOP, EXPERTS])
        disp = sb("disp", [TOK, TILES, EXPERTS])
        dT = sb("dT", [EXPERTS, ALL])
        D = sb("D", [128, EXPERTS // 2, ALL])

        ffn = sb("ffn", [128, EXPERTS // GROUP, FFN_COLS])
        whi = sb("whi", [128, 2, EXPERTS, HIDDEN], F32R)
        wlo = sb("wlo", [128, 2, EXPERTS, HIDDEN], F32R)
        sil = sb("sil", [HIDDEN, RING, ALL])
        hid = sb("hid", [HIDDEN, RING, ALL])
        prod = sb("prod", [128, PRING, ALL])
        acc = sb("acc", [128, 2, ALL])
        res = sb("res", [TOK, TILES, C])

        def part(name):
            rows, c0, n = SMALL[name]
            return small[0:rows, c0:c0 + n]

        tokb, lnb, g1col, qkvR, projR, g2row, b2row, scale_c, rel_rows, gate_w2, gate_row = (
            part(n) for n in ("tokb", "ln1_b", "ln1_g", "qkv", "proj", "ln2_g", "ln2_b", "scale", "rel",
                              "gate_w", "gate_b"))

        def raw12(e):
            return ffn[:, e // GROUP, 0:2 * GROUP * HIDDEN].rearrange(
                "p (i e h) -> p i e h", i=2, e=GROUP)[:, :, e % GROUP, :]

        def w3_of(e):
            c0 = 2 * GROUP * HIDDEN + (e % GROUP) * C
            return ffn[:, e // GROUP, c0:c0 + C]

        s_tokw, s_tokw2, s_small, s_out = sem("s_tokw"), sem("s_tokw2"), sem("s_small"), sem("s_out")
        s_img = [sem(f"s_img{t}") for t in range(TILES)]
        s_ffn = [sem(f"s_ffn{g}") for g in range(EXPERTS // GROUP)]
        warm_ready = sem("warm_ready")
        pool_const = sem("pool_const")
        ident_ready = sem("ident_ready")
        mask_ready = sem("mask_ready")
        ones_ready = sem("ones_ready")
        fold_ready = sem("fold_ready")
        lnL_ready = sem("lnL_ready")
        projX_ready = sem("projX_ready")
        wT_psum, wT_ready = sem("wT_psum"), sem("wT_ready")
        GV_psum, GV_ready = sem("GV_psum"), sem("GV_ready")
        conv_done, gelu_done, h0_done = sem("conv_done"), sem("gelu_done"), sem("h0_done")
        ve_ready, rstd_ready = sem("ve_ready"), sem("rstd_ready")
        h0b_ready = sem("h0b_ready")
        y_ready, yT_psum, yT_ready = sem("y_ready"), sem("yT_psum"), sem("yT_ready")
        Z_psum, Z_ready, V_psum, V_ready = sem("Z_psum"), sem("Z_ready"), sem("V_psum"), sem("V_ready")
        score_done, max_ready, exp_done = sem("score_done"), sem("max_ready"), sem("exp_done")
        PT_psum, PT_ready = sem("PT_psum"), sem("PT_ready")
        attn_done, x3_ready = sem("attn_done"), sem("x3_ready")
        xT_psum, xs_round, xs_ready = sem("xT_psum"), sem("xs_round"), sem("xs_ready")
        logit_done, gap_ready, tanh_done = sem("logit_done"), sem("gap_ready"), sem("tanh_done")
        disp_ready, dT_psum, dT_ready = sem("disp_ready"), sem("dT_psum"), sem("dT_ready")
        s_D = [sem(f"s_D{p}") for p in range(EXPERTS // 2)]
        whi_ready, wlo_ready = sem("whi_ready"), sem("wlo_ready")
        up1_done, up2_done, silu_done, hid_ready = sem("up1_done"), sem("up2_done"), sem("silu_done"), sem("hid_ready")
        down_done, prod_ready, acc_done = sem("down_done"), sem("prod_ready"), sem("acc_done")
        res_psum, res_ready = sem("res_psum"), sem("res_ready")
        dve_step = sem("dve_step")
        pool_step = sem("pool_step")

        out_dst = out.rearrange("(t i) n d -> (i n) t d", t=TILES)

        block = ctx.enter_context(nc.Block())

        @block.sync
        def _(sp):
            sp.dma_start(tokw[:, 0:FIRST_TAPS, :], tokw_in[:, 0:FIRST_TAPS, :]).then_inc(s_tokw, 16)
            for t in range(TILES):
                b = slice(t * TILE_IMAGES, (t + 1) * TILE_IMAGES)
                sp.dma_start(img[:, b, :], img_in[t]).then_inc(s_img[t], 16)
                if t == CHUNK - 1:
                    sp.dma_start(tokw[:, FIRST_TAPS:TAPS, :], tokw_in[:, FIRST_TAPS:TAPS, :]).then_inc(s_tokw2, 16)
                    sp.dma_start(small[:], small_in).then_inc(s_small, 16)
            for g in range(EXPERTS // GROUP):
                sp.dma_start(ffn[:, g, :], ffn_in[g]).then_inc(s_ffn[g], 16)
            sp.wait_ge(dT_ready, 1)
            for p in range(EXPERTS // 2):
                two_rows = dT[2 * p:2 * p + 2, :].rearrange("e (a n) -> e a n", a=1).to_broadcast([2, C, ALL])
                sp.dma_start(D[:, p, :], two_rows).then_inc(s_D[p], 16)
            sp.wait_ge(res_ready, CHUNKS)
            sp.dma_start(out_dst, res[:]).then_inc(s_out, 16)
            sp.wait_ge(s_out, 16)

        @block.gpsimd
        def _(pool):
            n_step = [0]

            def link(ins):
                n_step[0] += 1
                ins.then_inc(pool_step, 1)
                pool.wait_ge(pool_step, n_step[0])

            nc.gpsimd.memset(half_neg[:], -0.5)
            link(nc.gpsimd.memset(ident[:], 0.0))
            nc.gpsimd.affine_select(out=ident[:], in_=ident[:], compare_op=ALU.not_equal, fill=1.0, base=0,
                                    pattern=[[-1, 128]], channel_multiplier=1).then_inc(ident_ready, 1)
            nc.gpsimd.memset(ones_row[:], 1.0).then_inc(ones_ready, 1)
            pool.wait_ge(s_small, 16)
            rel_b = rel_rows.rearrange("p (a j) -> p a j", a=1).to_broadcast([TOK, TILE_IMAGES, SEQ])
            mask3 = relmask[:].rearrange("p (b j) -> p b j", j=SEQ)
            link(nc.gpsimd.affine_select(out=mask3, in_=rel_b, compare_op=ALU.is_ge, fill=MASKED, base=0,
                                         pattern=[[-SEQ, TILE_IMAGES], [0, SEQ]], channel_multiplier=1))
            nc.gpsimd.affine_select(out=mask3, in_=mask3, compare_op=ALU.is_ge, fill=MASKED, base=SEQ - 1,
                                    pattern=[[SEQ, TILE_IMAGES], [0, SEQ]], channel_multiplier=-1
                                    ).then_inc(mask_ready, 1)
            nc.gpsimd.iota(iota16[:], pattern=[[1, EXPERTS]], base=0, channel_multiplier=0,
                           allow_small_or_imprecise_dtypes=True).then_inc(pool_const, 1)

            def low_part(e):
                pool.wait_ge(whi_ready, e + 1)
                nc.gpsimd.tensor_tensor(wlo[:, :, e, :], raw12(e), whi[:, :, e, :].bitcast(F32),
                                        ALU.subtract).then_inc(wlo_ready, 1)

            def power(k, c, n):
                pool.wait_ge(ve_ready, n)
                t = slice(c * CHUNK, (c + 1) * CHUNK)
                nc.gpsimd.tensor_tensor(rstd[:, k, t], ve[:, k, t], half_neg[0:TOK, t],
                                        ALU.pow).then_inc(rstd_ready, 1)

            def add_pair(p):
                pool.wait_ge(prod_ready, p + 1)
                if p >= 2:
                    pool.wait_ge(acc_done, p - 1)
                before = prod[:, 0, :] if p == 1 else acc[:, (p - 1) % 2, :]
                nc.gpsimd.tensor_tensor(acc[:, p % 2, :], before, prod[:, p % PRING, :], ALU.add).then_inc(acc_done, 1)

            for n, (k, c) in enumerate(LN_ORDER):
                power(k, c, n + 1)
                for e in range(LOW_AFTER[n], LOW_AFTER[n + 1]):
                    low_part(e)
            for p in range(1, SUMMED):
                add_pair(p)

        @block.scalar
        def _(act):
            nc.scalar.preload_act_table(ACT.Gelu)
            act.wait_ge(s_small, 16)

            def round_weights(experts):
                for e in experts:
                    if e % GROUP == 0:
                        act.wait_ge(s_ffn[e // GROUP], 16)
                    nc.scalar.copy(whi[:, :, e, :], raw12(e)).then_inc(whi_ready, 1)

            for c in range(CHUNKS):
                act.wait_ge(conv_done, c + 1)
                nc.scalar.activation(gT[:, c, :], ps_a[c][:, 0:TOK], ACT.Gelu, bias=tokb
                                     ).then_inc(gelu_done, 1)
                if c == 0:
                    round_weights(range(0, ROUND[0]))
            nc.scalar.preload_act_table(ACT.Exp)
            round_weights(range(ROUND[0], ROUND[1]))
            for c in range(CHUNKS):
                t0 = c * CHUNK
                act.wait_ge(max_ready, c + 1)
                for t in range(CHUNK):
                    nc.scalar.activation(P[:, t0 + t, 0:TOK], ps_c[c][0:TOK, t * TOK:(t + 1) * TOK], ACT.Exp,
                                         bias=nmax[:, t0 + t:t0 + t + 1],
                                         accum_out=P[:, t0 + t, TOK:TOK + 1]).then_inc(exp_done, 1)
                act.wait_ge(V_psum, c + 1)
                nc.scalar.copy(V[0:TOK, t0:t0 + CHUNK, :], ps_b[c][0:TOK, 0:CHUNK * 2 * C].rearrange(
                    "p (t n) -> p t n", t=CHUNK)).then_inc(V_ready, 1)
                round_weights(range(ROUND[1 + c], ROUND[2 + c]))
            nc.scalar.preload_act_table(ACT.Silu)
            round_weights(range(ROUND[3], EXPERTS))
            for c in range(CHUNKS):
                act.wait_ge(xT_psum, c + 1)
                nc.scalar.copy(xs[:, c * CTOK:(c + 1) * CTOK], ps_b[c][:, 0:CTOK]).then_inc(xs_round, 1)

            for e in range(EXPERTS):
                act.wait_ge(up1_done, e + 1)
                if e >= RING:
                    act.wait_ge(hid_ready, e - RING + 1)
                nc.scalar.activation(sil[:, e % RING, :], ps_c[e % 2][:, 0:ALL], ACT.Silu).then_inc(silu_done, 1)
                if e == 3:
                    act.wait_ge(gap_ready, 1)
                    nc.scalar.activation(tnh[:], gap[:], ACT.Tanh, scale=0.5).then_inc(tanh_done, 1)

        @block.vector
        def _(dve):
            n_step = [0]

            def step(*instructions):
                for ins in instructions:
                    n_step[0] += 1
                    ins.then_inc(dve_step, 1)

            def caught_up():
                dve.wait_ge(dve_step, n_step[0])

            def link(*instructions):
                step(*instructions)
                caught_up()

            nc.vector.memset(warm[:], 0.0).then_inc(warm_ready, 1)
            nc.vector.memset(lnL[C:C + 1, 0:C], 0.0).then_inc(lnL_ready, 1)
            nc.vector.memset(lnL[C:C + 1, C:C + 1], 1.0).then_inc(lnL_ready, 1)
            nc.vector.memset(yT[C:C + 1, :], 1.0).then_inc(lnL_ready, 1)
            dve.wait_ge(ident_ready, 1)
            nc.vector.tensor_tensor(fold2[:], ident[:, 0:C], ident[:, C:128], ALU.add).then_inc(fold_ready, 1)
            dve.wait_ge(s_small, 16)
            nc.vector.tensor_copy(lnL[0:C, C:C + 1], lnb).then_inc(lnL_ready, 1)
            nc.vector.tensor_scalar(lnL[0:C, 0:C], ident[0:C, 0:C], g1col, None, ALU.mult
                                    ).then_inc(lnL_ready, 1)
            link(nc.vector.tensor_reduce(projm[:], projR, AX_X, ALU.add))
            link(nc.vector.tensor_scalar(projm[:], projm[:], 1.0 / C, None, ALU.mult))
            link(nc.vector.tensor_scalar(projX[:, 0:C], projR, projm[:, 0:1], None, ALU.subtract))
            nc.vector.tensor_tensor(projX[:, C:2 * C], projX[:, 0:C], g2row, ALU.mult).then_inc(projX_ready, 1)
            dve.wait_ge(wT_psum, 1)
            nc.vector.tensor_copy(wT[:], ps_p[0:C, 0:3 * (C + 1)].rearrange("p (i n) -> p i n", i=3)
                                  ).then_inc(wT_ready, 1)
            dve.wait_ge(GV_psum, 1)
            nc.vector.tensor_copy(G[:], ps_d[0:C + 1, 0:C + 1]).then_inc(GV_ready, 1)
            nc.vector.tensor_scalar(VW[:], ps_d[0:C + 1, 128:128 + 2 * C], scale_c[0:C + 1, :], None, ALU.mult
                                    ).then_inc(GV_ready, 1)
            nc.vector.tensor_copy(V[TOK:TOK + 1, :, :], projX[C:C + 1, :].rearrange("p (a n) -> p a n", a=1)
                                  .to_broadcast([1, TILES, 2 * C])).then_inc(GV_ready, 1)
            def bn(sources, k, c):
                t0 = c * CHUNK
                link(*[nc.vector.bn_stats(stats[:, k, t0 + t, :], sources[t]) for t in range(CHUNK)])
                link(*[nc.vector.bn_aggr(mv[:, k, t0 + t, :], stats[:, k, t0 + t, :]) for t in range(CHUNK)])

            def normal_stats(k, c, sources, mul, add):
                t0 = c * CHUNK
                bn(sources, k, c)
                nc.vector.tensor_scalar(ve[:, k, t0:t0 + CHUNK], mv[:, k, t0:t0 + CHUNK, 1], mul, add,
                                        ALU.mult, ALU.add).then_inc(ve_ready, 1)

            def h0_of(c):
                return [ps_a[c][0:TOK, 128 + t * C:128 + (t + 1) * C] for t in range(CHUNK)]

            def stats_in(c):
                dve.wait_ge(h0_done, c + 1)
                h0 = h0_of(c)
                normal_stats(0, c, h0, 1.0 + EPS, EPS * EPS)
                for t in range(CHUNK):
                    nc.vector.tensor_tensor(h0b[:, c * CHUNK + t, :], h0[t], b2row, ALU.add).then_inc(h0b_ready, 1)

            def norm_in(c):
                dve.wait_ge(rstd_ready, LN_ORDER.index((0, c)) + 1)
                for t in range(CHUNK):
                    g = c * CHUNK + t
                    nc.vector.tensor_scalar(y[:, g, :], h0_of(c)[t], mv[:, 0, g, 0:1], rstd[:, 0, g:g + 1],
                                            ALU.subtract, ALU.mult).then_inc(y_ready, 1)

            def copy_yT(c):
                dve.wait_ge(yT_psum, c + 1)
                nc.vector.tensor_copy(yT[0:C, c * CTOK:(c + 1) * CTOK], ps_a[c][0:C, 256:256 + CTOK]
                                      ).then_inc(yT_ready, 1)

            def copy_Z(c):
                dve.wait_ge(Z_psum, c + 1)
                nc.vector.tensor_copy(Z[:, c * CTOK:(c + 1) * CTOK], ps_a[c][0:C + 1, 0:CTOK]).then_inc(Z_ready, 1)

            def row_max(c):
                t0 = c * CHUNK
                dve.wait_ge(score_done, c + 1)
                nc.vector.tensor_reduce(nmax[:, t0:t0 + CHUNK],
                                        ps_c[c][0:TOK, 0:CTOK].rearrange("p (t m) -> p t m", t=CHUNK),
                                        AX_X, ALU.max, negate=True).then_inc(max_ready, 1)

            def square_sums(c):
                t = slice(c * CHUNK, (c + 1) * CHUNK)
                dve.wait_ge(exp_done, CHUNK * (c + 1))
                step(nc.vector.scalar_tensor_tensor(eps_sum2[:, t], P[:, t, TOK], EPS, P[:, t, TOK],
                                                    ALU.mult, ALU.mult))

            def copy_PT(c):
                t0 = c * CHUNK
                dve.wait_ge(PT_psum, c + 1)
                nc.vector.tensor_copy(PT[:, t0:t0 + CHUNK, :], ps_a[c][0:TOK + 1, 0:CTOK].rearrange(
                    "p (t m) -> p t m", t=CHUNK)).then_inc(PT_ready, 1)

            def attn_of(c):
                return [ps_o[c][0:TOK, t * 2 * C:t * 2 * C + 2 * C] for t in range(CHUNK)]

            def stats_out(c):
                dve.wait_ge(attn_done, c + 1)
                t0 = c * CHUNK
                bn([v[:, 0:C] for v in attn_of(c)], 1, c)
                nc.vector.tensor_tensor(ve[:, 1, t0:t0 + CHUNK], mv[:, 1, t0:t0 + CHUNK, 1],
                                        eps_sum2[:, t0:t0 + CHUNK], ALU.add).then_inc(ve_ready, 1)

            def residual(c):
                t0 = c * CHUNK
                dve.wait_ge(h0b_ready, CHUNK * (c + 1))
                dve.wait_ge(rstd_ready, LN_ORDER.index((1, c)) + 1)
                step(*[nc.vector.scalar_tensor_tensor(h1[:, t0 + t, :], attn_of(c)[t][:, C:2 * C],
                                                      rstd[:, 1, t0 + t:t0 + t + 1], h0b[:, t0 + t, :],
                                                      ALU.mult, ALU.add) for t in range(CHUNK)])

            def stats_x(c):
                t0 = c * CHUNK
                caught_up()
                normal_stats(2, c, [h1[:, t0 + t, :] for t in range(CHUNK)], 1.0, EPS)

            def norm_x(c):
                dve.wait_ge(rstd_ready, LN_ORDER.index((2, c)) + 1)
                for t in range(CHUNK):
                    g = c * CHUNK + t
                    nc.vector.tensor_scalar(x3[:, g, :, :], h1[:, g:g + 1, :].to_broadcast([TOK, 2, C]),
                                            mv[:, 2, g, 0:1], rstd[:, 2, g:g + 1], ALU.subtract, ALU.mult
                                            ).then_inc(x3_ready, 1)

            def split_x(c):
                cols = slice(c * CTOK, (c + 1) * CTOK)
                dve.wait_ge(xs_round, c + 1)
                nc.vector.tensor_tensor(xs[C:128, cols], ps_b[c][C:128, 0:CTOK], xs[C:128, cols].bitcast(F32),
                                        ALU.subtract).then_inc(xs_ready, 1)

            stats_in(0)
            norm_in(0)
            copy_yT(0)
            stats_in(1)
            copy_Z(0)
            norm_in(1)
            row_max(0)
            copy_yT(1)
            square_sums(0)
            copy_Z(1)
            copy_PT(0)
            row_max(1)
            stats_out(0)
            square_sums(1)
            copy_PT(1)
            residual(0)
            stats_out(1)
            stats_x(0)
            residual(1)
            stats_x(1)
            norm_x(0)
            norm_x(1)
            split_x(0)
            split_x(1)

            def hidden(e):
                dve.wait_ge(silu_done, e + 1)
                dve.wait_ge(up2_done, e + 1)
                if e >= RING:
                    dve.wait_ge(down_done, (e - RING) // 2 + 1)
                nc.vector.tensor_tensor(hid[:, e % RING, :], ps_a[e % 2][:, 0:ALL], sil[:, e % RING, :], ALU.mult
                                        ).then_inc(hid_ready, 1)

            def weigh(p):
                dve.wait_ge(down_done, p + 1)
                dve.wait_ge(s_D[p], 16)
                if p >= PRING:
                    dve.wait_ge(acc_done, max(p - PRING, 1))
                nc.vector.tensor_tensor(prod[:, p % PRING, :], ps_y[p % 4][:, 0:ALL], D[:, p, :], ALU.mult
                                        ).then_inc(prod_ready, 1)

            hidden(0)
            dve.wait_ge(logit_done, 1)
            lg = ps_p[0:TOK, 0:TILES * EXPERTS].rearrange("p (t e) -> p t e", t=TILES)
            step(*[nc.vector.max(top8[:, t, :], lg[:, t, :]) for t in range(TILES)])
            hidden(1)
            caught_up()
            nc.vector.tensor_tensor(gap[:], top8[:, :, 0], top8[:, :, 1], ALU.subtract).then_inc(gap_ready, 1)
            step(*[nc.vector.max_index(idx8[:, t, :], top8[:, t, :], lg[:, t, :]) for t in range(TILES)])
            caught_up()
            dve.wait_ge(pool_const, 1)
            step(*[nc.vector.tensor_tensor(
                hot[:, :, k, :],
                iota16[:].rearrange("p (a e) -> p a e", a=1).to_broadcast([TOK, TILES, EXPERTS]),
                idx8[:, :, k:k + 1].to_broadcast([TOK, TILES, EXPERTS]), ALU.is_equal) for k in range(TOP)])
            dve.wait_ge(tanh_done, 1)
            step(nc.vector.tensor_scalar(wtop[:, :, 0], tnh[:], 0.5, 0.5, ALU.mult, ALU.add),
                 nc.vector.tensor_scalar(wtop[:, :, 1], tnh[:], -0.5, 0.5, ALU.mult, ALU.add))
            hidden(2)
            caught_up()
            step(*[nc.vector.tensor_tensor(hot[:, :, k, :], hot[:, :, k, :],
                                           wtop[:, :, k:k + 1].to_broadcast([TOK, TILES, EXPERTS]), ALU.mult)
                   for k in range(TOP)])
            hidden(3)
            caught_up()
            nc.vector.tensor_tensor(disp[:], hot[:, :, 0, :], hot[:, :, 1, :], ALU.add).then_inc(disp_ready, 1)
            hidden(4)
            hidden(5)
            dve.wait_ge(dT_psum, 1)
            nc.vector.tensor_copy(dT[:], ps_p[0:EXPERTS, 0:ALL]).then_inc(dT_ready, 1)
            for e in range(6, EXPERTS):
                hidden(e)
                for p in pairs_after(e, WEIGH_AFTER):
                    weigh(p)
                    if p == SUMMED:
                        dve.wait_ge(acc_done, SUMMED - 1)
                        dve.wait_ge(prod_ready, SUMMED + 1)
                        nc.vector.tensor_tensor(acc[:, SUMMED % 2, :], acc[:, (SUMMED - 1) % 2, :],
                                                prod[:, SUMMED % PRING, :], ALU.add).then_inc(acc_done, 1)
            for c in range(CHUNKS):
                t0 = c * CHUNK
                dve.wait_ge(res_psum, c + 1)
                nc.vector.tensor_tensor(res[:, t0:t0 + CHUNK, :],
                                        ps_c[c][0:TOK, 0:CHUNK * C].rearrange("p (t d) -> p t d", t=CHUNK),
                                        h1[:, t0:t0 + CHUNK, :], ALU.add).then_inc(res_ready, 1)

        @block.tensor
        def _(pe):
            mm = nc.tensor.matmul

            def keep_clock(n, free_bank, columns=512):
                for _ in range(n):
                    mm(free_bank[:, 0:columns], warm[:, 0:128], warm[:, 0:columns], start=True, stop=True)

            pe.wait_ge(warm_ready, 1)
            keep_clock(ZEROS_START, ps_b[1])

            def fold_maps():
                pe.wait_ge(lnL_ready, 5)
                for i in range(3):
                    last = mm(ps_p[0:C, i * (C + 1):(i + 1) * (C + 1)], qkvR[:, i * C:(i + 1) * C], lnL[:],
                              start=True, stop=True)
                last.then_inc(wT_psum, 1)

            def join_maps():
                pe.wait_ge(wT_ready, 1)
                pe.wait_ge(projX_ready, 1)
                mm(ps_d[0:C + 1, 0:C + 1], wT[:, 0, :], wT[:, 1, :], start=True, stop=True)
                mm(ps_d[0:C + 1, 128:128 + 2 * C], wT[:, 2, :], projX[0:C, :], start=True, stop=True
                   ).then_inc(GV_psum, 1)

            def conv(c, taps):
                if taps[0] == 0:
                    for t in range(CHUNK):
                        pe.wait_ge(s_img[c * CHUNK + t], 16)
                for j in taps:
                    k = 128 if j < TAPS - 1 else C
                    for t in range(CHUNK):
                        b0 = (c * CHUNK + t) * TILE_IMAGES
                        patch = img[0:k, b0:b0 + TILE_IMAGES, j:j + HSTEP * (SEQ - 1) + 1:HSTEP]
                        last = mm(ps_a[c][t * C:(t + 1) * C, 0:TOK].rearrange("p (b n) -> p b n", n=SEQ),
                                  tokw[0:k, j, :], patch, start=(j == 0), stop=(j == TAPS - 1))
                if taps[-1] == TAPS - 1:
                    last.then_inc(conv_done, 1)

            def to_tokens(c):
                pe.wait_ge(gelu_done, c + 1)
                nc.tensor.transpose(ps_a[c][0:TOK, 128:256], gT[:, c, :], ident[:]).then_inc(h0_done, 1)

            def y_to_T(c):
                pe.wait_ge(y_ready, CHUNK * (c + 1))
                for t in range(CHUNK):
                    last = nc.tensor.transpose(ps_a[c][0:C, 256 + t * TOK:256 + (t + 1) * TOK],
                                               y[:, c * CHUNK + t, :], ident[0:TOK, 0:TOK])
                last.then_inc(yT_psum, 1)

            def project(c):
                cols = slice(c * CTOK, (c + 1) * CTOK)
                pe.wait_ge(yT_ready, c + 1)
                mm(ps_a[c][0:C + 1, 0:CTOK], G[:], yT[:, cols], start=True, stop=True).then_inc(Z_psum, 1)

            def values(c):
                for t in range(CHUNK):
                    tok = slice(c * CTOK + t * TOK, c * CTOK + (t + 1) * TOK)
                    last = mm(ps_b[c][0:TOK, t * 2 * C:(t + 1) * 2 * C], yT[:, tok], VW[:], start=True, stop=True)
                last.then_inc(V_psum, 1)

            def scores(c):
                pe.wait_ge(Z_ready, c + 1)
                for t in range(CHUNK):
                    tok = slice(c * CTOK + t * TOK, c * CTOK + (t + 1) * TOK)
                    last = mm(ps_c[c][0:TOK, t * TOK:(t + 1) * TOK], Z[:, tok], yT[:, tok],
                              start=False, stop=(t == CHUNK - 1), skip_group_check=True)
                last.then_inc(score_done, 1)

            def P_to_T(c):
                pe.wait_ge(exp_done, CHUNK * (c + 1))
                for t in range(CHUNK):
                    last = nc.tensor.transpose(ps_a[c][0:TOK + 1, t * TOK:(t + 1) * TOK], P[:, c * CHUNK + t, :],
                                               ident[0:TOK, 0:TOK])
                last.then_inc(PT_psum, 1)

            def attend(c):
                pe.wait_ge(PT_ready, c + 1)
                pe.wait_ge(V_ready, c + 1)
                for t in range(CHUNK):
                    last = mm(ps_o[c][0:TOK, t * 2 * C:(t + 1) * 2 * C], PT[:, c * CHUNK + t, :],
                              V[:, c * CHUNK + t, :], start=True, stop=True)
                last.then_inc(attn_done, 1)

            def x_to_T(c):
                pe.wait_ge(x3_ready, CHUNK * (c + 1))
                for t in range(CHUNK):
                    last = nc.tensor.transpose(ps_b[c][:, t * TOK:(t + 1) * TOK],
                                               x3[:, c * CHUNK + t, :, :].rearrange("p a d -> p (a d)"),
                                               ident[0:TOK, 0:TOK])
                last.then_inc(xT_psum, 1)

            pe.wait_ge(s_tokw, 16)
            conv(0, range(FIRST_TAPS))
            pe.wait_ge(s_tokw2, 16)
            conv(0, range(FIRST_TAPS, FOLD_TAP))
            fold_maps()
            conv(0, range(FOLD_TAP, TAPS))
            join_maps()
            conv(1, range(3))
            to_tokens(0)
            conv(1, range(3, TAPS))
            pe.wait_ge(GV_ready, 3)
            y_to_T(0)
            to_tokens(1)
            pe.wait_ge(mask_ready, 1)
            for c in range(CHUNKS):
                two = relmask[:].rearrange("p (a m) -> p a m", a=1).to_broadcast([TOK, CHUNK, TOK])
                mm(ps_c[c][0:TOK, 0:CTOK].rearrange("p (t m) -> p t m", t=CHUNK), ident[0:TOK, 0:TOK], two,
                   start=True, stop=False, skip_group_check=True)
            project(0)
            values(0)
            keep_clock(ZEROS_ATTENTION[0], ps_d, 256)
            scores(0)
            keep_clock(ZEROS_ATTENTION[1], ps_d, 256)
            y_to_T(1)
            keep_clock(ZEROS_ATTENTION[2], ps_d, 256)
            project(1)
            P_to_T(0)
            keep_clock(ZEROS_ATTENTION[3], ps_d, 256)
            scores(1)
            attend(0)
            values(1)
            P_to_T(1)
            attend(1)
            keep_clock(ZEROS_EXPERTS[0], ps_c[0])
            x_to_T(0)
            keep_clock(ZEROS_EXPERTS[1], ps_c[0])
            x_to_T(1)

            def logits(c):
                if c == 0:
                    gate_b4 = gate_row.rearrange("p (a e) -> p a e", a=1).to_broadcast([1, TILES, EXPERTS])
                    mm(ps_p[0:TOK, 0:TILES * EXPERTS].rearrange("p (t e) -> p t e", t=TILES), ones_row[:], gate_b4,
                       start=True, stop=False, skip_group_check=True)
                for t in range(c * CHUNK, (c + 1) * CHUNK):
                    last = mm(ps_p[0:TOK, t * EXPERTS:(t + 1) * EXPERTS],
                              xs[:, t * TOK:(t + 1) * TOK].bitcast(F32), gate_w2,
                              start=False, stop=(t == TILES - 1), skip_group_check=True)
                if c == CHUNKS - 1:
                    last.then_inc(logit_done, 1)

            def up(i, e, dst, done, cols=slice(0, ALL)):
                pe.wait_ge(whi_ready, e + 1)
                pe.wait_ge(wlo_ready, e + 1)
                mm(dst[:, cols], whi[:, i, e, :], xs[:, cols], start=True, stop=False)
                last = mm(dst[:, cols], wlo[:, i, e, :], xs[:, cols], start=False, stop=True)
                if cols.stop == ALL:
                    last.then_inc(done, 1)

            def up1(e):
                if e >= 2:
                    pe.wait_ge(silu_done, e - 1)
                up(0, e, ps_c[e % 2], up1_done)

            def up2(e):
                if e >= 2:
                    pe.wait_ge(hid_ready, e - 1)
                up(1, e, ps_a[e % 2], up2_done)

            def down(p):
                pe.wait_ge(s_ffn[2 * p // GROUP], 16)
                pe.wait_ge(hid_ready, 2 * p + 2)
                if p >= 4:
                    pe.wait_ge(prod_ready, p - 3)
                if p == 3:
                    pe.wait_ge(dT_ready, 1)
                for h in range(2):
                    e = 2 * p + h
                    last = mm(ps_y[p % 4][h * C:(h + 1) * C, 0:ALL], w3_of(e), hid[:, e % RING, :],
                              start=True, stop=True)
                last.then_inc(down_done, 1)

            def dispatch_to_T():
                pe.wait_ge(disp_ready, 1)
                for t in range(TILES):
                    last = nc.tensor.transpose(ps_p[0:EXPERTS, t * TOK:(t + 1) * TOK], disp[:, t, :],
                                               ident[0:TOK, 0:TOK])
                last.then_inc(dT_psum, 1)

            pe.wait_ge(ones_ready, 1)
            for c in range(CHUNKS):
                cols = slice(c * CTOK, (c + 1) * CTOK)
                pe.wait_ge(xs_ready, c + 1)
                if c == 0:
                    logits(c)
                up(0, 0, ps_c[0], up1_done, cols)
                up(0, 1, ps_c[1], up1_done, cols)
            for e in range(EXPERTS):
                up2(e)
                if e == 0:
                    logits(1)
                if e + 2 < EXPERTS:
                    up1(e + 2)
                if e == 5:
                    dispatch_to_T()
                for p in pairs_after(e):
                    down(p)
            folds = ((acc_done, SUMMED, acc[:, SUMMED % 2, :]),
                     (prod_ready, SUMMED + 2, prod[:, (SUMMED + 1) % PRING, :]))
            pe.wait_ge(fold_ready, 1)
            for i, (done, n, part_sum) in enumerate(folds):
                pe.wait_ge(done, n)
                for t in range(TILES):
                    c, k = divmod(t, CHUNK)
                    last = mm(ps_c[c][0:TOK, k * C:(k + 1) * C], part_sum[:, t * TOK:(t + 1) * TOK], fold2[:],
                              start=(i == 0 and k == 0), stop=(i == len(folds) - 1 and k == CHUNK - 1),
                              skip_group_check=True)
                    if i == len(folds) - 1 and k == CHUNK - 1:
                        last.then_inc(res_psum, 1)


def pairs_after(e, when=DOWN_AFTER):
    return [p for p, at in enumerate(when) if at == e]


LN_ORDER = [(0, 0), (0, 1), (1, 0), (1, 1), (2, 0), (2, 1)]
LOW_AFTER = [0, 3, 9, 9, 9, 10, EXPERTS]


_OUT = (IMAGES, SEQ, C)


def kernel(**inputs):
    import numpy as np
    from concourse import bacc
    from concourse.bass_utils import run_bass_kernel_spmd

    a = {k.replace("L0_", ""): np.asarray(v) for k, v in inputs.items()}

    def by_parity(v):
        odd = np.concatenate([v[..., 1::2], np.zeros_like(v[..., :1])], axis=-1)
        return v[..., 0::2], odd

    rows = a["x"][:, 0, 0:PH, 0:COLS].reshape(TILES, TILE_IMAGES, PH, COLS).transpose(0, 2, 1, 3)
    img = np.concatenate(by_parity(rows), axis=1)
    taps = a["tok_weight"].reshape(PH, PW, C).transpose(0, 2, 1)
    tokw = np.concatenate(by_parity(taps), axis=0).transpose(0, 2, 1)

    table = a["attn_bias_table"]
    rel = np.stack([table[SEQ - 1 - i:2 * SEQ - 1 - i] for i in range(SEQ)])
    pieces = {
        "tokb": np.tile(a["tok_bias"], 2)[:, None],
        "ln1_b": a["attn_ln1_b"][:, None],
        "ln1_g": a["attn_ln1_g"][:, None],
        "scale": np.broadcast_to(a["attn_scale"], (TOK, 1)),
        "qkv": np.concatenate([a["attn_qkv_w"], a["attn_qkv_b"][None]]),
        "proj": np.concatenate([a["attn_proj_w"], a["attn_proj_b"][None]]),
        "ln2_g": np.broadcast_to(a["attn_ln2_g"], (C + 1, C)),
        "ln2_b": np.broadcast_to(a["attn_ln2_b"], (TOK, C)),
        "rel": np.tile(rel, (TILE_IMAGES, 1)),
        "gate_w": np.tile(a["ffn_gate_w"], (2, 1)),
        "gate_b": a["ffn_gate_b"][None],
    }
    small = np.zeros((128, SMALL_COLS), np.float32)
    for name, (n, c0, cols) in SMALL.items():
        small[0:n, c0:c0 + cols] = pieces[name]

    groups = EXPERTS // GROUP
    up = np.stack([a["ffn_w1"], a["ffn_w2"]]).reshape(2, groups, GROUP, C, HIDDEN).transpose(1, 3, 0, 2, 4)
    up = np.tile(up.reshape(groups, C, 2 * GROUP * HIDDEN), (1, 2, 1))
    down = a["ffn_w3"].reshape(groups, GROUP, HIDDEN, C).transpose(0, 2, 1, 3).reshape(groups, HIDDEN, GROUP * C)
    ffn = np.concatenate([up, down], axis=2)

    nc = bacc.Bacc("TRN2", target_bir_lowering=False, num_devices=1)
    arrays, args = {}, []
    for name, v in (("img", img), ("tokw", tokw), ("small", small), ("ffn", ffn)):
        arrays[f"in_{name}"] = np.ascontiguousarray(v)
        args.append(nc.dram_tensor(f"in_{name}", v.shape, F32, kind="ExternalInput").ap())
    args.append(nc.dram_tensor("out_dram", _OUT, F32, kind="ExternalOutput").ap())
    vit_tower(nc, *args)
    r = run_bass_kernel_spmd(nc, [arrays], core_ids=[0])
    return r.results[0]["out_dram"]
```
